# Optimizing a Trainium2 kernel written in Bass

```python
import numpy as np
import jax
import jax.numpy as jnp

def _softmax(x, axis=-1):
    return jax.nn.softmax(x, axis=axis)

def _gelu(x):
    return jax.nn.gelu(x, approximate=True)

def _silu(x):
    return jax.nn.silu(x)

def _sigmoid(x):
    return jax.nn.sigmoid(x)

def _layernorm(x, axis=-1, eps=1e-05):
    m = jnp.mean(x, axis=axis, keepdims=True)
    v = jnp.var(x, axis=axis, keepdims=True)
    return (x - m) / jnp.sqrt(v + eps)

def _scatter_add(tgt, idx, src, axis=0):
    return tgt.at[idx].add(src)

def _segment_sum(src, seg, n):
    return jax.ops.segment_sum(src, seg, n)
kernel_name = 'mk_adaln_ffn_d1_seqx_r2_54912a'

def setup_inputs(seed: int=0):
    np.random.seed(seed)
    _w = jnp.asarray

    def _rec_inputs():
        import jax
        import jax.numpy as jnp
        _rk = jax.random.key(seed)
        x = -7.109e-05 + 0.9999 * jax.random.normal(jax.random.fold_in(_rk, 1), (8, 512, 512), jnp.float32)
        _lenS = 512 - jax.random.randint(jax.random.fold_in(_rk, 7), (8,), 0, max(1, 512 // 4) + 1, jnp.int32)
        _lenS2 = 512 - jax.random.randint(jax.random.fold_in(_rk, 8), (8,), 0, max(1, 512 // 4) + 1, jnp.int32)
        cond_512 = 0.0061147 + 1.02565 * jax.random.normal(jax.random.fold_in(_rk, 11), (8, 256), jnp.float32)
        return (x, cond_512)
    x, cond_512 = _rec_inputs()

    def _L0_cond_setup():
        import jax, jax.numpy as jnp
        import numpy as np
        W_DIM = 256
        CLAMP = 256.0
        key = jax.random.key(seed)
        ks = jax.random.split(key, 6)
        B, L, C = (8, 4096, 512)
        return {'x': jax.random.normal(ks[0], (B, L, C), dtype=jnp.float32), 'w': jax.random.normal(ks[1], (B, W_DIM), dtype=jnp.float32), 'weight': jax.random.normal(ks[2], (C, C), dtype=jnp.float32), 'bias': jax.random.normal(ks[3], (C,), dtype=jnp.float32), 'affine_w': jax.random.normal(ks[4], (C, W_DIM), dtype=jnp.float32), 'affine_b': jnp.ones((C,), dtype=jnp.float32)}
    _L0_cond_all = _L0_cond_setup()
    _L0_cond_in = {k: v for k, v in _L0_cond_all.items() if k in ('weight', 'bias', 'affine_w', 'affine_b')}
    del _L0_cond_all

    def _L0_ffn_setup():
        import jax, jax.numpy as jnp
        import numpy as np
        from math import ceil
        CAPACITY_FACTOR = 2.0
        MIN_CAPACITY = 4
        key = jax.random.key(seed)
        ks = jax.random.split(key, 4)
        B, S, D, Di, E = (4, 1024, 512, 2048, 8)
        x = jax.random.normal(ks[0], (B, S, D), dtype=jnp.float32)
        Wr = jax.random.normal(ks[1], (D, E), dtype=jnp.float32) * D ** (-0.5)
        W1 = jax.random.normal(ks[2], (E, D, Di), dtype=jnp.float32) * D ** (-0.5)
        b1 = jnp.zeros((E, Di), dtype=jnp.float32)
        W2 = jax.random.normal(ks[3], (E, Di, D), dtype=jnp.float32) * Di ** (-0.5)
        b2 = jnp.zeros((E, D), dtype=jnp.float32)
        return {'x': x, 'Wr': Wr, 'W1': W1, 'b1': b1, 'W2': W2, 'b2': b2}
    _L0_ffn_all = _L0_ffn_setup()
    _L0_ffn_in = {k: v for k, v in _L0_ffn_all.items() if k in ('Wr', 'W1', 'b1', 'W2', 'b2')}
    del _L0_ffn_all
    return {'x': x, 'cond_512': cond_512, 'L0_cond_weight': _L0_cond_in['weight'], 'L0_cond_bias': _L0_cond_in['bias'], 'L0_cond_affine_w': _L0_cond_in['affine_w'], 'L0_cond_affine_b': _L0_cond_in['affine_b'], 'L0_ffn_Wr': _L0_ffn_in['Wr'], 'L0_ffn_W1': _L0_ffn_in['W1'], 'L0_ffn_b1': _L0_ffn_in['b1'], 'L0_ffn_W2': _L0_ffn_in['W2'], 'L0_ffn_b2': _L0_ffn_in['b2']}

def reference(x, cond_512, L0_cond_weight, L0_cond_bias, L0_cond_affine_w, L0_cond_affine_b, L0_ffn_Wr, L0_ffn_W1, L0_ffn_b1, L0_ffn_W2, L0_ffn_b2):
    import jax
    import jax.numpy as jnp

    def _L0_cond_ref(x, w, weight, bias, affine_w, affine_b):
        import jax, jax.numpy as jnp
        import numpy as np
        W_DIM = 256
        CLAMP = 256.0
        B, L, C = x.shape
        gain = 1.0 / np.sqrt(W_DIM).astype(np.float32)
        styles = w @ (affine_w * gain).T + affine_b
        ws = weight[None, :, :] * styles[:, None, :]
        dcoefs = jax.lax.rsqrt(jnp.sum(ws * ws, axis=2) + 1e-08)
        xm = x * styles[:, None, :]
        y = jnp.einsum('blc,oc->blo', xm, weight)
        y = y * dcoefs[:, None, :]
        y = jnp.clip(y + bias, -CLAMP, CLAMP)
        return y

    def _L0_ffn_ref(x, Wr, W1, b1, W2, b2):
        import jax, jax.numpy as jnp
        import numpy as np
        from math import ceil
        CAPACITY_FACTOR = 2.0
        MIN_CAPACITY = 4
        B, S, D = x.shape
        E = Wr.shape[1]
        N = B * S
        k = max(MIN_CAPACITY, ceil(N * CAPACITY_FACTOR / E))
        xt = x.reshape(N, D)
        scores = jax.nn.softmax(xt @ Wr, axis=-1)
        G, idx = jax.lax.top_k(scores.T, k)
        X_in = xt[idx]
        h = jax.nn.gelu(jnp.einsum('ekd,edh->ekh', X_in, W1) + b1[:, None, :], approximate=False)
        X_e = jnp.einsum('ekh,ehd->ekd', h, W2) + b2[:, None, :]
        contrib = (G[..., None] * X_e).reshape(E * k, D)
        out = jnp.zeros((N, D), dtype=x.dtype).at[idx.reshape(-1)].add(contrib)
        return out.reshape(B, S, D)
    x = x + _L0_ffn_ref(_L0_cond_ref(x, cond_512, L0_cond_weight, L0_cond_bias, L0_cond_affine_w, L0_cond_affine_b), L0_ffn_Wr, L0_ffn_W1, L0_ffn_b1, L0_ffn_W2, L0_ffn_b2)
    return x

_drawn_inputs = setup_inputs


def setup_inputs(seed=0):
    import zlib

    import numpy as np

    out = dict(_drawn_inputs(seed))
    spreads = {'L0_cond_affine_b': (1.0, 0.2), 'L0_ffn_b1': (0.0, 0.272), 'L0_ffn_b2': (0.0, 0.1)}
    factors = {}
    for name, (base, spread) in spreads.items():
        noise = np.random.default_rng([zlib.crc32(name.encode()), seed]).standard_normal(out[name].shape)
        drawn = base * np.exp(spread * noise) if base else spread * noise
        out[name] = jnp.asarray(drawn.astype(out[name].dtype))
    for name, factor in factors.items():
        out[name] = (out[name] * factor).astype(out[name].dtype)
    return out
```

```python
import concourse.bass as bass
from concourse import mybir
from contextlib import ExitStack


def adaln_moe_kernel(nc, xT, x, condT, WT, biasT, affWT, affbT, WrT, W1, b1T, W2, b2, out):
    f32 = mybir.dt.float32
    f32r = mybir.dt.float32r
    bf16 = mybir.dt.bfloat16
    i32 = mybir.dt.int32
    u32 = mybir.dt.uint32
    ALU = mybir.AluOpType
    ACT = mybir.ActivationFunctionType
    AX = mybir.AxisListType

    NB = 8
    NT = 32
    E = 8
    K = 1024
    NU = 2 * E
    NJ = 16
    NBLK = NU * NJ
    CLAMP = 256.0

    y_d = nc.dram_tensor("y_rows", (NT * 128, 512), f32, kind="Internal").ap()

    ctx = ExitStack()
    with ctx:
        def sb(name, shape, dt):
            return ctx.enter_context(nc.sbuf_tensor(name, shape, dt))

        def pb(name):
            return ctx.enter_context(nc.psum_tensor(name, [128, 512], f32))

        def sem(name):
            return ctx.enter_context(nc.semaphore(name))

        R = sb("Rraw", [128, NJ, 1024], f32)
        W1S = sb("W1S", [128, 3, 2, 512], f32r)
        W2S = sb("W2S", [128, 3, 2, 512], f32r)
        XT = sb("XT", [128, 2, 2, 4, 512], f32r)
        HS = sb("HS", [128, 3, 2, 512], f32r)
        HF = sb("HF", [128, 2, 512], f32)
        XR = sb("XR", [128, 4, 512], f32)
        OB = sb("OB", [128, 4, 512], f32)
        B2 = sb("B2", [128, 2, 512], f32)
        OH = sb("OH", [128, 2, 8, 128], bf16)
        RH = sb("RH", [128, 5, NT, 8], bf16)
        V = sb("V", [128, 5, NT, 8], bf16)
        HM = sb("HM", [128, NT, 8], bf16)
        S = sb("S", [128, NT, E], f32)
        S2 = sb("S2", [128, 256], f32)
        slo = sb("slo", [128, NT, E], i32)
        shi = sb("shi", [128, NT, E], i32)
        ident = sb("ident", [128, 128], f32)
        io128 = sb("io128", [128, 128], f32)
        BO = sb("BO", [128, 128], bf16)
        TRI = sb("TRI", [128, 128], bf16)
        b1 = sb("b1", [128, E * NJ], f32)
        idx = sb("idx", [128, E, 8], u32)
        G = sb("G", [128, E, 8], f32)
        IM = sb("IM", [128, 40], f32)
        idf = sb("idf", [128, 8], f32)
        gs = sb("gs", [128, 8], f32)
        cand = sb("cand", [128, 1], i32)
        mbit = sb("mbit", [128, 1], i32)
        cnt = sb("cnt", [128, 1], bf16)
        r1 = sb("r1", [128, 4], bf16)
        r2 = sb("r2", [128, 4], bf16)
        r3 = sb("r3", [128, 4], bf16)
        offs = sb("offs", [128, 4], f32)
        affb = sb("affb", [128, 4], f32)
        biasc = sb("biasc", [128, 4], f32)
        wr = sb("wr", [128, 4, E], f32)
        cT = sb("cT", [128, 2, NB], f32)
        sty = sb("sty", [128, 4, NB], f32)
        sty2 = sb("sty2", [128, 4, NB], f32)
        dv = sb("dv", [128, 4, NB], f32)
        dsq = sb("dsq", [128, 4, NB], f32)
        dr = sb("dr", [128, 4, NB], f32)
        de = sb("de", [128, 4, NB], f32)
        dco = sb("dco", [128, 4, NB], f32)
        mx = sb("mx", [128, 4], f32)
        lg = sb("lg", [128, 4, E], f32)
        ex = sb("ex", [128, 4, E], f32)
        sm = sb("sm", [128, 4], f32)
        rs = sb("rs", [128, 4], f32)

        def slot2(s):
            return R[:, s:s + 2, :].rearrange("p s n -> p (s n)").rearrange("p (c n) -> p c n", c=4)

        XB = [slot2(14), slot2(12)]
        YT = [slot2(10), slot2(8)]
        WTraw = slot2(6)
        WSQ = slot2(4)
        AWT = R[:, 2, :].rearrange("p (k n) -> p k n", k=2)
        sg = R[:, 3, 0:256]
        se = R[:, 3, 256:512]
        mg = R[:, 3, 512:768]
        me = R[:, 3, 768:1024]
        sa = R[:, 4, 0:256]
        sbq = R[:, 4, 256:512]
        junk = R[:, 4, 512:768]
        sr = R[:, 5, 0:256]
        sr2 = R[:, 5, 256:512]
        sli = sb("sli", [128, NT * E], i32)
        Jt = sb("Jt", [128, 128], i32)
        Jm = sb("Jm", [128, 128], i32)

        BB = [pb(f"BB{i}") for i in range(4)]
        AB = [pb(f"AB{i}") for i in range(2)]
        TB = pb("TB")
        IB = pb("IB")

        def wt(hl, c):
            return W1S[:, c, hl, :] if c < 3 else W2S[:, 0, hl, :]

        def asf(ap):
            return ap.bitcast(f32)

        s_c = {n: sem(f"s_c_{n}") for n in ("aff", "small", "wt", "bias", "b1")}
        s_x = [sem(f"s_x{i}") for i in range(2)]
        s_id = sem("s_id")
        s_cst = sem("s_cst")
        s_sp = sem("s_sp")
        s_sty = sem("s_sty")
        s_wsq = sem("s_wsq")
        s_dp = sem("s_dp")
        s_dvv = sem("s_dvv")
        s_dsq = sem("s_dsq")
        s_dco = sem("s_dco")
        s_wth = sem("s_wth")
        s_wtl = sem("s_wtl")
        s_xmh = sem("s_xmh")
        s_xml = sem("s_xml")
        s_cp = sem("s_cp")
        s_ce = sem("s_ce")
        s_cl = sem("s_cl")
        s_rt = sem("s_rt")
        s_lg = sem("s_lg")
        s_ex = sem("s_ex")
        s_S = sem("s_S")
        s_yt = sem("s_yt")
        s_yra = sem("s_yra")
        s_yrv = sem("s_yrv")
        s_yd = [sem(f"s_yd{i}") for i in range(4)]
        s_o0 = sem("s_o0")
        s_s2t = sem("s_s2t")
        s_s2 = sem("s_s2")
        s_cnt = sem("s_cnt")
        s_pc = sem("s_pc")
        s_rr = sem("s_rr")
        s_off = sem("s_off")
        s_slot = sem("s_slot")
        s_slt = sem("s_slt")
        s_sli = sem("s_sli")
        s_V = sem("s_V")
        s_v = sem("s_v")
        s_p = sem("s_p")
        s_R = sem("s_R")
        s_oh = sem("s_oh")
        s_im = sem("s_im")
        s_imc = sem("s_imc")
        s_idx = sem("s_idx")
        s_raw = [sem(f"s_raw{j}") for j in range(NJ)]
        s_w1h = sem("s_w1h")
        s_w1l = sem("s_w1l")
        s_w2h = sem("s_w2h")
        s_w2l = sem("s_w2l")
        s_A = sem("s_A")
        s_B = sem("s_B")
        s_Bt = sem("s_Bt")
        s_g = sem("s_g")
        s_hl = sem("s_hl")
        s_ev = sem("s_ev")
        s_ob = sem("s_ob")
        s_sc = sem("s_sc")
        s_gat = [sem(f"s_gat{i}") for i in range(4)]
        s_T = sem("s_T")
        s_xh = sem("s_xh")
        s_xl = sem("s_xl")
        s_b2 = [sem(f"s_b2{i}") for i in range(2)]

        block = ctx.enter_context(nc.Block())

        @block.sync
        def _(eng):
            eng.dma_start(AWT, affWT).then_inc(s_c["aff"], 16)
            eng.dma_start(cT[:, :, :], condT).then_inc(s_c["aff"], 16)
            eng.dma_start(affb[:, :], affbT).then_inc(s_c["aff"], 16)
            eng.dma_start(WTraw, WT).then_inc(s_c["wt"], 16)
            eng.dma_start(XB[0], xT[0]).then_inc(s_x[0], 16)
            eng.dma_start(XB[1], xT[1]).then_inc(s_x[1], 16)
            eng.dma_start(biasc[:, :], biasT).then_inc(s_c["bias"], 16)
            eng.dma_start(wr[:, :, :], WrT).then_inc(s_c["small"], 16)
            eng.dma_start(b1[:, :], b1T).then_inc(s_c["b1"], 16)

            def load_w(e, j):
                eng.dma_start(R[:, j, 0:512], W1[e, j]).then_inc(s_raw[j], 16)
                eng.dma_start(R[:, j, 512:1024], W2[e, j]).then_inc(s_raw[j], 16)

            def load_b2(e):
                eng.dma_start(B2[:, e % 2, :], b2[e:e + 1, :].broadcast_to([128, 512])).then_inc(s_b2[e % 2], 16)

            load_w(0, 0)
            load_w(0, 1)
            load_b2(0)
            load_b2(1)

            def store_rows(b):
                for t in range(4 * b, 4 * b + 4):
                    if t % 2 == 0:
                        eng.wait_ge(s_yra, t // 2 + 1)
                    else:
                        eng.wait_ge(s_yrv, t // 2 + 1)
                    eng.dma_start(y_d[128 * t:128 * t + 128, :], OB[:, t % 4, :]).then_inc(s_yd[t % 4], 16)

            for b in range(2, NB):
                eng.wait_ge(s_xmh, 4 * (b - 1))
                eng.wait_ge(s_xml, 4 * (b - 1))
                eng.dma_start(XB[b % 2], xT[b]).then_inc(s_x[b % 2], 16)
                if b >= 3:
                    store_rows(b - 3)
            for b in range(NB - 3, NB):
                store_rows(b)
            eng.wait_ge(s_yt, NT)
            eng.wait_ge(s_rt, NB)
            eng.wait_ge(s_wth, 4)
            eng.wait_ge(s_wtl, 4)
            for j in list(range(6, NJ)) + [2]:
                load_w(0, j)
            eng.wait_ge(s_slt, 1)
            eng.wait_ge(s_V, 1)
            for j in range(3, 6):
                load_w(0, j)
            for e in range(1, E):
                for j in range(NJ):
                    eng.wait_ge(s_w2h, 32 * (e - 1) + 16 + j + 1)
                    eng.wait_ge(s_w2l, 32 * (e - 1) + 16 + j + 1)
                    load_w(e, j)
                    if e >= 2 and j == 4:
                        eng.wait_ge(s_ev, 8 * (e - 1))
                        load_b2(e)
            for i in range(4):
                eng.wait_ge(s_yd[i], 16 * 8)
            eng.wait_ge(s_sc, 64 * NU)

        @block.gpsimd
        def _(eng):
            eng.memset(ident[:, :], 0.0).then_inc(s_p, 1)
            eng.wait_ge(s_p, 1)
            eng.affine_select(out=ident[:, :], in_=ident[:, :], compare_op=ALU.not_equal, fill=1.0,
                              base=0, pattern=[[-1, 128]], channel_multiplier=1).then_inc(s_id, 1)
            eng.iota(io128[:, :], pattern=[[1, 128]], base=0, channel_multiplier=0,
                     allow_small_or_imprecise_dtypes=True).then_inc(s_cst, 1)
            eng.iota(Jt[:, :], pattern=[[1, 128]], base=128, channel_multiplier=-1).then_inc(s_cst, 1)
            eng.iota(V[:, 0, :, :], pattern=[[0, 256]], base=0, channel_multiplier=1,
                     allow_small_or_imprecise_dtypes=True).then_inc(s_cst, 1)
            eng.iota(V[:, 1, :, :], pattern=[[1, NT], [0, 8]], base=0, channel_multiplier=0,
                     allow_small_or_imprecise_dtypes=True).then_inc(s_cst, 1)
            eng.wait_ge(s_xmh, 4 * (NB - 1))
            eng.dma_start(out.rearrange("(a b) d -> a (b d)", a=512), x.rearrange("(a b) d -> a (b d)", a=512)).then_inc(s_o0, 16)
            Sf = S[:, :, :].rearrange("p t e -> p (t e)")
            Vf = [V[:, i, :, :].rearrange("p t e -> p (t e)") for i in range(5)]
            eng.wait_ge(s_S, NB)
            eng.wait_ge(s_wsq, 1)
            eng.wait_ge(s_dp, 1)
            eng.tensor_copy(Vf[2], Sf).then_inc(s_p, 1)
            eng.wait_ge(s_p, 2)
            eng.tensor_tensor(sr, Sf, Vf[2], ALU.subtract).then_inc(s_p, 1)
            eng.wait_ge(s_p, 3)
            eng.tensor_copy(Vf[3], sr).then_inc(s_p, 1)
            eng.wait_ge(s_p, 4)
            eng.tensor_tensor(sr2, sr, Vf[3], ALU.subtract).then_inc(s_p, 1)
            eng.wait_ge(s_p, 5)
            eng.tensor_copy(Vf[4], sr2).then_inc(s_V, 1)

            def gather(u):
                eng.wait_ge(s_idx, u // 2 + 1)
                for t in range(4):
                    c = 4 * (u % 2) + t
                    if u:
                        eng.wait_ge(s_T, 4 * (u - 1) + t + 1)
                    eng.indirect_dma_start(
                        XR[:, t, :], None, y_d[:, :],
                        bass.IndirectOffsetOnAxis(idx[:, u // 2, c:c + 1], 0),
                        bounds_check=NT * 128 - 1, oob_is_err=True).then_inc(s_gat[t], 16)

            def scatter(u):
                if u == 0:
                    eng.wait_ge(s_o0, 16)
                else:
                    eng.wait_ge(s_sc, 64 * u)
                for t in range(4):
                    c = 4 * (u % 2) + t
                    eng.wait_ge(s_ob, 4 * u + t + 1)
                    eng.indirect_dma_start(
                        out[:, :], bass.IndirectOffsetOnAxis(idx[:, u // 2, c:c + 1], 0),
                        OB[:, t, :], None,
                        bounds_check=NT * 128 - 1, oob_is_err=True,
                        compute_op=ALU.add).then_inc(s_sc, 16)

            for i in range(4):
                eng.wait_ge(s_yd[i], 16 * 8)
            gather(0)
            gather(1)
            for u in range(NU):
                scatter(u)
                if u + 2 < NU:
                    gather(u + 2)

        @block.scalar
        def _(eng):
            eng.wait_ge(s_c["wt"], 16)
            eng.activation(WSQ, WTraw, ACT.Square).then_inc(s_wsq, 1)
            for c in range(4):
                eng.activation(wt(0, c), WTraw[:, c, :], ACT.Copy).then_inc(s_wth, 1)
            eng.wait_ge(s_sty, 1)

            def xm_hi(b):
                eng.wait_ge(s_x[b % 2], 16 * (b // 2 + 1))
                if b >= 2:
                    eng.wait_ge(s_cp, 4 * (b - 1))
                for c in range(4):
                    eng.activation(XT[:, b % 2, 0, c, :], XB[b % 2][:, c, :], ACT.Copy,
                                   scale=sty[:, c, b:b + 1]).then_inc(s_xmh, 1)

            def row_evac(t):
                eng.wait_ge(s_yt, t + 1)
                if t >= 4:
                    eng.wait_ge(s_yd[t % 4], 16 * (t // 4))
                eng.activation(OB[:, t % 4, :], TB[:, :], ACT.Copy).then_inc(s_yra, 1)

            xm_hi(0)
            xm_hi(1)
            eng.wait_ge(s_dvv, 1)
            eng.activation(dsq[:, :, :], dv[:, :, :], ACT.Sqrt).then_inc(s_dsq, 1)
            eng.wait_ge(s_dco, 1)
            eng.wait_ge(s_c["bias"], 16)
            for b in range(NB + 1):
                if b < NB:
                    for o in range(4):
                        eng.wait_ge(s_cp, 4 * b + o + 1)
                        if b >= 2:
                            eng.wait_ge(s_rt, b - 1)
                            eng.wait_ge(s_yt, 4 * (b - 1))
                        eng.activation(YT[b % 2][:, o, :], BB[o][:, :], ACT.Identity,
                                       scale=dco[:, o, b:b + 1], bias=biasc[:, o:o + 1]).then_inc(s_ce, 1)
                    if b + 2 < NB:
                        xm_hi(b + 2)
                if b >= 1:
                    eng.wait_ge(s_lg, b)
                    eng.activation(ex[:, :, :], lg[:, :, :], ACT.Exp).then_inc(s_ex, 1)
                    row_evac(4 * (b - 1))
                    row_evac(4 * (b - 1) + 2)

            def w1_hi(i):
                j = i % NJ
                eng.wait_ge(s_raw[j], 32 * (i // 32 + 1))
                if i >= 3:
                    eng.wait_ge(s_A, i - 2)
                elif i < 3:
                    eng.wait_ge(s_cp, 4 * NB)
                eng.activation(W1S[:, i % 3, 0, :], R[:, j, 0:512], ACT.Copy).then_inc(s_w1h, 1)

            def w2_hi(i):
                j = i % NJ
                eng.wait_ge(s_raw[j], 32 * (i // 32 + 1))
                if i >= 3:
                    eng.wait_ge(s_B, i - 2)
                eng.activation(W2S[:, i % 3, 0, :], R[:, j, 512:1024], ACT.Copy).then_inc(s_w2h, 1)

            def x_hi(u, t):
                n = 4 * u + t
                eng.wait_ge(s_T, n + 1)
                eng.activation(XT[:, u % 2, 0, :, 128 * t:128 * t + 128],
                               TB[:, :].rearrange("p (c n) -> p c n", c=4), ACT.Copy).then_inc(s_xh, 1)

            w1_hi(0)
            w1_hi(1)
            for t in range(4):
                x_hi(0, t)
            for i in range(NBLK):
                if i + 2 < NBLK:
                    w1_hi(i + 2)
                w2_hi(i)
                eng.wait_ge(s_A, i + 1)
                if i >= 2:
                    eng.wait_ge(s_hl, i - 1)
                bias = b1[:, (i // 32) * NJ + i % NJ:(i // 32) * NJ + i % NJ + 1]
                if i == 0:
                    eng.wait_ge(s_c["b1"], 16)
                eng.activation(HF[:, i % 2, :], AB[i % 2][:, :], ACT.Gelu, bias=bias)
                eng.activation(HS[:, i % 3, 0, :], AB[i % 2][:, :], ACT.Gelu, bias=bias).then_inc(s_g, 1)
                u, j = i // NJ, i % NJ
                if u + 1 < NU and j in (4, 6, 8, 10):
                    x_hi(u + 1, (j - 4) // 2)

        @block.vector
        def _(eng):
            chain = [0]

            def link(ins):
                chain[0] += 1
                ins.then_inc(s_v, 1)
                eng.wait_ge(s_v, chain[0])

            eng.wait_ge(s_c["wt"], 16)
            eng.wait_ge(s_c["aff"], 48)
            eng.wait_ge(s_sp, 1)
            link(eng.scalar_tensor_tensor(sty[:, :, :], IB[:, 0:32].rearrange("p (c b) -> p c b", c=4), 1.0 / 16.0,
                                          affb[:, :, None].broadcast_to([128, 4, NB]), ALU.mult, ALU.add))
            eng.tensor_tensor(sty2[:, :, :], sty[:, :, :], sty[:, :, :], ALU.mult).then_inc(s_sty, 1)
            for c in range(4):
                eng.wait_ge(s_wth, c + 1)
                eng.tensor_tensor(wt(1, c), WTraw[:, c, :], asf(wt(0, c)), ALU.subtract).then_inc(s_wtl, 1)

            def xm_lo(b):
                eng.wait_ge(s_x[b % 2], 16 * (b // 2 + 1))
                for c in range(4):
                    eng.wait_ge(s_xmh, 4 * b + c + 1)
                    eng.scalar_tensor_tensor(XT[:, b % 2, 1, c, :], XB[b % 2][:, c, :], sty[:, c, b:b + 1],
                                             asf(XT[:, b % 2, 0, c, :]), ALU.mult, ALU.subtract).then_inc(s_xml, 1)

            xm_lo(0)
            eng.wait_ge(s_dp, 1)
            eng.tensor_scalar(dv[:, :, :], TB[:, 0:32].rearrange("p (c b) -> p c b", c=4), 1e-8, None,
                              ALU.add).then_inc(s_dvv, 1)
            xm_lo(1)
            eng.wait_ge(s_dsq, 1)
            link(eng.reciprocal(dr[:, :, :], dsq[:, :, :]))
            link(eng.tensor_tensor(de[:, :, :], dv[:, :, :], dr[:, :, :], ALU.mult))
            link(eng.tensor_tensor(de[:, :, :], de[:, :, :], dr[:, :, :], ALU.mult))
            link(eng.tensor_scalar(de[:, :, :], de[:, :, :], -0.5, 1.5, ALU.mult, ALU.add))
            eng.tensor_tensor(dco[:, :, :], dr[:, :, :], de[:, :, :], ALU.mult).then_inc(s_dco, 1)
            eng.wait_ge(s_cst, 4)
            link(eng.tensor_scalar(Jm[:, :], Jt[:, :], 7, None, ALU.bitwise_and))
            link(eng.tensor_scalar(BO[:, :], Jm[:, :], 0.0, None, ALU.is_equal))
            link(eng.scalar_tensor_tensor(TRI[:, :], Jt[:, :], 128.0, BO[:, :], ALU.is_gt, ALU.mult))

            def row_evac(t):
                eng.wait_ge(s_yt, t + 1)
                if t >= 4:
                    eng.wait_ge(s_yd[t % 4], 16 * (t // 4))
                eng.tensor_copy(OB[:, t % 4, :], IB[:, :]).then_inc(s_yrv, 1)

            for b in range(NB + 1):
                if b < NB:
                    for o in range(4):
                        eng.wait_ge(s_ce, 4 * b + o + 1)
                        yv = YT[b % 2][:, o, :]
                        eng.tensor_scalar(yv, yv, -CLAMP, CLAMP, ALU.max, ALU.min).then_inc(s_cl, 1)
                    if b + 2 < NB:
                        xm_lo(b + 2)
                if b >= 1:
                    q = b - 1
                    eng.wait_ge(s_rt, q + 1)
                    L = AB[q % 2][:, 0:32].rearrange("p (t e) -> p t e", t=4)
                    link(eng.tensor_reduce(mx[:, :], L, AX.X, ALU.max))
                    if q:
                        eng.wait_ge(s_ex, q)
                    eng.tensor_tensor(lg[:, :, :], L, mx[:, :, None].broadcast_to([128, 4, E]),
                                      ALU.subtract).then_inc(s_lg, 1)
                    if b < NB:
                        row_evac(4 * q + 1)
                        row_evac(4 * q + 3)
                    eng.wait_ge(s_ex, q + 1)
                    link(eng.tensor_reduce(sm[:, :], ex[:, :, :], AX.X, ALU.add))
                    link(eng.reciprocal(rs[:, :], sm[:, :]))
                    eng.tensor_tensor(S[:, 4 * q:4 * q + 4, :], ex[:, :, :],
                                      rs[:, :, None].broadcast_to([128, 4, E]), ALU.mult).then_inc(s_S, 1)
                    if b == NB:
                        row_evac(4 * q + 1)
                        row_evac(4 * q + 3)

            eng.memset(cand[:, :], 1 << 29)
            eng.wait_ge(s_s2t, 1)
            link(eng.tensor_copy(S2[:, :], AB[0][:, 0:256]))
            for n, bit in enumerate(range(29, -1, -1)):
                eng.tensor_scalar(junk, S2[:, :], cand[:, :].bitcast(f32), None, ALU.is_ge, ALU.add,
                                  accum_out=cnt[:, :]).then_inc(s_cnt, 1)
                eng.wait_ge(s_pc, n + 1)
                link(eng.tensor_scalar(mbit[:, :], AB[1][:, 0:1], float(K), float(1 << bit), ALU.is_lt, ALU.mult))
                half = (1 << (bit - 1)) if bit else 0
                link(eng.scalar_tensor_tensor(cand[:, :], mbit[:, :], half, cand[:, :],
                                              ALU.bitwise_or, ALU.bitwise_xor))
            thr = cand[:, :].bitcast(f32)
            eng.tensor_scalar(mg, S2[:, :], thr, None, ALU.is_gt)
            link(eng.tensor_scalar(me, S2[:, :], thr, None, ALU.is_equal))
            for h in range(2):
                q = slice(128 * h, 128 * h + 128)
                eng.tensor_tensor_scan(sg[:, q], mg[:, q], mg[:, q], 0.0, ALU.add, ALU.max)
                last = eng.tensor_tensor_scan(se[:, q], me[:, q], me[:, q], 0.0, ALU.add, ALU.max)
            link(last)
            eng.memset(r2[:, :], 0.0)
            eng.memset(r3[:, :], 0.0)
            eng.tensor_copy(r1[:, 0:2], sg[:, 127:256:128])
            link(eng.tensor_copy(r1[:, 2:4], se[:, 127:256:128]))
            eng.tensor_copy(r2[:, 1:4:2], r1[:, 0:4:2])
            link(eng.tensor_tensor(r3[:, 2:3], r1[:, 0:1], r1[:, 1:2], ALU.add))
            eng.tensor_copy(r3[:, 3:4], r3[:, 2:3]).then_inc(s_rr, 1)
            eng.wait_ge(s_off, 1)
            link(eng.tensor_copy(offs[:, :], AB[1][:, 0:4]))
            for h in range(2):
                q = slice(128 * h, 128 * h + 128)
                eng.scalar_tensor_tensor(sa[:, q], sg[:, q], offs[:, h:h + 1], mg[:, q], ALU.add, ALU.mult)
                last = eng.scalar_tensor_tensor(sbq[:, q], se[:, q], offs[:, 2 + h:3 + h], me[:, q], ALU.add, ALU.mult)
            link(last)
            eng.tensor_tensor(sa, sa, sbq, ALU.add).then_inc(s_slot, 1)
            eng.wait_ge(s_slt, 1)
            link(eng.tensor_scalar(sli[:, :], AB[0][:, 0:256], -1.0, None, ALU.add))
            eng.tensor_scalar(slo[:, :, :].rearrange("p t e -> p (t e)"), sli[:, :], 127, None, ALU.bitwise_and)
            link(eng.tensor_scalar(shi[:, :, :].rearrange("p t e -> p (t e)"), sli[:, :], 7, None,
                                   ALU.arith_shift_right))
            eng.wait_ge(s_V, 1)

            def build_rhs(e):
                if e:
                    eng.wait_ge(s_im, 4 * e)
                link(eng.tensor_tensor(HM[:, :, :], shi[:, :, e:e + 1].broadcast_to([128, NT, 8]),
                                       io128[:, None, 0:8].broadcast_to([128, NT, 8]), ALU.is_equal))
                eng.tensor_tensor(RH[:, :, :, :], V[:, :, :, e:e + 1].broadcast_to([128, 5, NT, 8]),
                                  HM[:, None, :, :].broadcast_to([128, 5, NT, 8]), ALU.mult).then_inc(s_R, 1)

            def build_oh(e, q):
                n = 4 * e + q
                if n >= 2:
                    eng.wait_ge(s_im, n - 1)
                eng.tensor_tensor(OH[:, n % 2, :, :],
                                  slo[:, 8 * q:8 * q + 8, e:e + 1].broadcast_to([128, 8, 128]),
                                  io128[:, None, :].broadcast_to([128, 8, 128]), ALU.is_equal).then_inc(s_oh, 1)

            def finish_idx(e):
                eng.wait_ge(s_im, 4 * e + 4)
                eng.tensor_copy(IM[:, :], IB[:, 0:40]).then_inc(s_imc, 1)
                eng.wait_ge(s_imc, e + 1)
                link(eng.scalar_tensor_tensor(idf[:, :], IM[:, 8:16], 128.0, IM[:, 0:8], ALU.mult, ALU.add))
                eng.tensor_tensor(gs[:, :], IM[:, 16:24], IM[:, 24:32], ALU.add)
                link(eng.tensor_copy(idx[:, e, :], idf[:, :]))
                eng.tensor_tensor(G[:, e, :], gs[:, :], IM[:, 32:40], ALU.add).then_inc(s_idx, 1)

            build_rhs(0)
            for q in range(4):
                build_oh(0, q)
            finish_idx(0)

            def w1_lo(i):
                eng.wait_ge(s_w1h, i + 1)
                eng.tensor_tensor(W1S[:, i % 3, 1, :], R[:, i % NJ, 0:512], asf(W1S[:, i % 3, 0, :]),
                                  ALU.subtract).then_inc(s_w1l, 1)

            def w2_lo(i):
                eng.wait_ge(s_w2h, i + 1)
                eng.tensor_tensor(W2S[:, i % 3, 1, :], R[:, i % NJ, 512:1024], asf(W2S[:, i % 3, 0, :]),
                                  ALU.subtract).then_inc(s_w2l, 1)

            def x_lo(u, t):
                n = 4 * u + t
                eng.wait_ge(s_T, n + 1)
                eng.wait_ge(s_xh, n + 1)
                q = slice(128 * t, 128 * t + 128)
                eng.tensor_tensor(XT[:, u % 2, 1, :, q], TB[:, :].rearrange("p (c n) -> p c n", c=4),
                                  asf(XT[:, u % 2, 0, :, q]), ALU.subtract).then_inc(s_xl, 1)

            def evac_add(u):
                e = u // 2
                eng.wait_ge(s_b2[e % 2], 16 * (e // 2 + 1))
                if u == 0:
                    for t in range(4):
                        eng.wait_ge(s_yd[t], 16 * 8)
                else:
                    eng.wait_ge(s_sc, 64 * u)
                for t in range(4):
                    eng.wait_ge(s_Bt, 4 * u + t + 1)
                    eng.tensor_tensor(OB[:, t, :], BB[t][:, :], B2[:, e % 2, :], ALU.add).then_inc(s_ev, 1)

            def evac_mul(u):
                e = u // 2
                for t in range(4):
                    c = 4 * (u % 2) + t
                    eng.wait_ge(s_ev, 4 * u + t + 1)
                    eng.tensor_scalar(OB[:, t, :], OB[:, t, :], G[:, e, c:c + 1], None, ALU.mult).then_inc(s_ob, 1)

            w1_lo(0)
            w1_lo(1)
            for t in range(4):
                x_lo(0, t)
            for i in range(NBLK + 2):
                if i + 2 < NBLK:
                    w1_lo(i + 2)
                if i < NBLK:
                    w2_lo(i)
                    eng.wait_ge(s_g, i + 1)
                    eng.tensor_tensor(HS[:, i % 3, 1, :], HF[:, i % 2, :], asf(HS[:, i % 3, 0, :]),
                                      ALU.subtract).then_inc(s_hl, 1)
                u, j = i // NJ, i % NJ
                if u >= 1 and j == 1:
                    evac_add(u - 1)
                if u >= 1 and j == 2 and i < NBLK:
                    evac_mul(u - 1)
                if i == NBLK + 1:
                    evac_mul(NU - 1)
                if u + 1 < NU and j in (4, 6, 8, 10):
                    x_lo(u + 1, (j - 4) // 2)
                if u % 2 == 0 and u + 2 < NU:
                    e = u // 2 + 1
                    if j == 3:
                        build_rhs(e)
                    if j in (5, 7, 9, 11):
                        build_oh(e, (j - 5) // 2)
                    if j == 13:
                        finish_idx(e)

        @block.tensor
        def _(eng):
            mm = nc.tensor.matmul
            eng.wait_ge(s_c["aff"], 48)
            for c in range(4):
                for k in range(2):
                    last = mm(IB[:, 8 * c:8 * c + 8], AWT[:, k, 128 * c:128 * c + 128], cT[:, k, :],
                              start=(k == 0), stop=(k == 1))
            last.then_inc(s_sp, 1)
            eng.wait_ge(s_sty, 1)
            eng.wait_ge(s_wsq, 1)
            for o in range(4):
                for c in range(4):
                    last = mm(TB[:, 8 * o:8 * o + 8], WSQ[:, c, 128 * o:128 * o + 128], sty2[:, c, :],
                              start=(c == 0), stop=(c == 3))
            last.then_inc(s_dp, 1)
            eng.wait_ge(s_wth, 4)
            eng.wait_ge(s_wtl, 4)

            def cond(b):
                eng.wait_ge(s_xmh, 4 * b + 4)
                eng.wait_ge(s_xml, 4 * b + 4)
                for o in range(4):
                    if b:
                        eng.wait_ge(s_ce, 4 * (b - 1) + o + 1)
                    for c in range(4):
                        for n, (a, d) in enumerate(((0, 0), (0, 1), (1, 0))):
                            last = mm(BB[o][:, :], wt(a, c)[:, 128 * o:128 * o + 128], XT[:, b % 2, d, c, :],
                                      start=(c == 0 and n == 0), stop=(c == 3 and n == 2))
                    last.then_inc(s_cp, 1)

            def router(b):
                eng.wait_ge(s_cl, 4 * b + 4)
                if b == 0:
                    eng.wait_ge(s_c["small"], 16)
                if b >= 2:
                    eng.wait_ge(s_lg, b - 1)
                for t in range(4):
                    for c in range(4):
                        last = mm(AB[b % 2][:, 8 * t:8 * t + 8], YT[b % 2][:, c, 128 * t:128 * t + 128],
                                  wr[:, c, :], start=(c == 0), stop=(c == 3))
                last.then_inc(s_rt, 1)

            def rows(b):
                for t in range(4 * b, 4 * b + 4):
                    bank = TB if t % 2 == 0 else IB
                    if t >= 2:
                        eng.wait_ge(s_yra if t % 2 == 0 else s_yrv, t // 2)
                    if t == 0:
                        eng.wait_ge(s_id, 1)
                        eng.wait_ge(s_dvv, 1)
                    q = slice(128 * (t - 4 * b), 128 * (t - 4 * b) + 128)
                    for c in range(4):
                        last = nc.tensor.transpose(bank[:, 128 * c:128 * c + 128], YT[b % 2][:, c, q], ident[:, :])
                    last.then_inc(s_yt, 1)

            cond(0)
            for b in range(1, NB + 1):
                if b < NB:
                    cond(b)
                router(b - 1)
                rows(b - 1)
            eng.wait_ge(s_S, NB)
            for h in range(2):
                last = nc.tensor.transpose(AB[0][:, 128 * h:128 * h + 128],
                                           S[:, 16 * h:16 * h + 16, :].rearrange("p t e -> p (t e)"), ident[:, :])
            last.then_inc(s_s2t, 1)
            for n in range(30):
                eng.wait_ge(s_cnt, n + 1)
                mm(AB[1][:, 0:1], BO[:, :], cnt[:, :], start=True, stop=True).then_inc(s_pc, 1)
            eng.wait_ge(s_rr, 1)
            mm(AB[1][:, 0:4], TRI[:, :], r1[:, :], start=True, stop=False)
            mm(AB[1][:, 0:4], BO[:, :], r2[:, :], start=False, stop=False)
            mm(AB[1][:, 0:4], BO[:, :], r3[:, :], start=False, stop=True).then_inc(s_off, 1)
            eng.wait_ge(s_slot, 1)
            for h in range(2):
                last = nc.tensor.transpose(AB[0][:, 128 * h:128 * h + 128], sa[:, 128 * h:128 * h + 128], ident[:, :])
            last.then_inc(s_slt, 1)

            def lists(e, q):
                if q == 0:
                    eng.wait_ge(s_R, e + 1)
                    if e:
                        eng.wait_ge(s_imc, e)
                    else:
                        eng.wait_ge(s_yrv, NT // 2)
                eng.wait_ge(s_oh, 4 * e + q + 1)
                for k in range(8):
                    t = 8 * q + k
                    last = mm(IB[:, 0:40].rearrange("p (v h) -> p v h", v=5), OH[:, (4 * e + q) % 2, k, :],
                              RH[:, :, t, :], start=(t == 0), stop=(t == NT - 1))
                last.then_inc(s_im, 1)

            def x_transpose(u, t):
                n = 4 * u + t
                eng.wait_ge(s_gat[t], 16 * (u + 1))
                if n:
                    eng.wait_ge(s_xl, n)
                else:
                    eng.wait_ge(s_yra, NT // 2)
                for c in range(4):
                    last = nc.tensor.transpose(TB[:, 128 * c:128 * c + 128], XR[:, t, 128 * c:128 * c + 128],
                                               ident[:, :])
                last.then_inc(s_T, 1)

            def A(i):
                u = i // NJ
                if i % NJ == 0:
                    eng.wait_ge(s_xh, 4 * u + 4)
                    eng.wait_ge(s_xl, 4 * u + 4)
                if i >= 2:
                    eng.wait_ge(s_g, i - 1)
                eng.wait_ge(s_w1h, i + 1)
                eng.wait_ge(s_w1l, i + 1)
                for c in range(4):
                    for n, (a, d) in enumerate(((0, 0), (0, 1), (1, 0))):
                        last = mm(AB[i % 2][:, :], W1S[:, i % 3, a, 128 * c:128 * c + 128], XT[:, u % 2, d, c, :],
                                  start=(c == 0 and n == 0), stop=(c == 3 and n == 2))
                last.then_inc(s_A, 1)

            def B(i):
                u, j = i // NJ, i % NJ
                eng.wait_ge(s_w2h, i + 1)
                eng.wait_ge(s_w2l, i + 1)
                eng.wait_ge(s_g, i + 1)
                eng.wait_ge(s_hl, i + 1)
                for t in range(4):
                    if j == 0 and u:
                        eng.wait_ge(s_ev, 4 * (u - 1) + t + 1)
                    for n, (a, d) in enumerate(((0, 0), (0, 1), (1, 0))):
                        last = mm(BB[t][:, :], HS[:, i % 3, a, 128 * t:128 * t + 128], W2S[:, i % 3, d, :],
                                  start=(j == 0 and n == 0), stop=(j == NJ - 1 and n == 2))
                    if j == NJ - 1:
                        last.then_inc(s_Bt, 1)
                if j == NJ - 1:
                    eng.wait_ge(s_Bt, 4 * u + 4)
                    eng.sem_inc(s_B, 1)
                else:
                    last.then_inc(s_B, 1)

            for q in range(4):
                lists(0, q)
            for t in range(4):
                x_transpose(0, t)
            for i in range(NBLK + 2):
                if i < NBLK:
                    A(i)
                u, j = i // NJ, i % NJ
                if u + 1 < NU and j in (4, 6, 8, 10):
                    x_transpose(u + 1, (j - 4) // 2)
                if u % 2 == 0 and u + 2 < NU and j in (5, 7, 9, 11):
                    lists(u // 2 + 1, (j - 5) // 2)
                if i >= 2:
                    B(i - 2)


_OUT = (8, 512, 512)


def kernel(x, cond_512, L0_cond_weight, L0_cond_bias, L0_cond_affine_w, L0_cond_affine_b, L0_ffn_Wr,
           L0_ffn_W1, L0_ffn_b1, L0_ffn_W2, L0_ffn_b2):
    import numpy as np
    import concourse.bacc as bacc
    from concourse import mybir
    from concourse.bass_utils import run_bass_kernel_spmd

    def chunks(a, n):
        a = np.asarray(a)
        return np.ascontiguousarray(a.reshape(n, 128, -1).transpose(1, 0, 2))

    x = np.asarray(x)
    arrays = {
        "xT": np.ascontiguousarray(x.reshape(8, 512, 4, 128).transpose(0, 3, 2, 1)),
        "x": np.ascontiguousarray(x.reshape(4096, 512)),
        "condT": chunks(np.asarray(cond_512).T, 2),
        "WT": chunks(np.asarray(L0_cond_weight).T, 4),
        "biasT": np.ascontiguousarray(np.asarray(L0_cond_bias).reshape(4, 128).T),
        "affWT": chunks(np.asarray(L0_cond_affine_w).T, 2),
        "affbT": np.ascontiguousarray(np.asarray(L0_cond_affine_b).reshape(4, 128).T),
        "WrT": chunks(L0_ffn_Wr, 4),
        "W1": np.ascontiguousarray(
            np.asarray(L0_ffn_W1).reshape(8, 4, 128, 16, 128).transpose(0, 3, 2, 1, 4)).reshape(8, 16, 128, 512),
        "b1T": np.ascontiguousarray(np.asarray(L0_ffn_b1).reshape(8, 16, 128).transpose(2, 0, 1)).reshape(128, 128),
        "W2": np.ascontiguousarray(np.asarray(L0_ffn_W2).reshape(8, 16, 128, 512)),
        "b2": np.ascontiguousarray(np.asarray(L0_ffn_b2)),
    }
    nc = bacc.Bacc("TRN2", target_bir_lowering=False, num_devices=1)
    f32 = mybir.dt.float32
    args = {n: nc.dram_tensor(f"in_{n}", a.shape, f32, kind="ExternalInput").ap() for n, a in arrays.items()}
    out = nc.dram_tensor("out_0", (4096, 512), f32, kind="ExternalOutput").ap()
    adaln_moe_kernel(nc, out=out, **args)
    r = run_bass_kernel_spmd(nc, [{f"in_{n}": a for n, a in arrays.items()}], core_ids=[0])
    return r.results[0]["out_0"].reshape(_OUT)
```

```python
import concourse.bass as bass
from concourse import mybir
from contextlib import ExitStack


def adaln_moe_kernel(nc, xT, x, condT, WT, biasT, affWT, affbT, WrT, W1, b1T, W2, b2, out):
    f32 = mybir.dt.float32
    f32r = mybir.dt.float32r
    bf16 = mybir.dt.bfloat16
    i32 = mybir.dt.int32
    u32 = mybir.dt.uint32
    ALU = mybir.AluOpType
    ACT = mybir.ActivationFunctionType
    AX = mybir.AxisListType

    NB = 8
    NT = 32
    E = 8
    K = 1024
    NU = 2 * E
    NJ = 16
    NBLK = NU * NJ
    CLAMP = 256.0

    y_d = nc.dram_tensor("y_rows", (NT * 128, 1024), f32, kind="Internal").ap()

    ctx = ExitStack()
    with ctx:
        def sb(name, shape, dt):
            return ctx.enter_context(nc.sbuf_tensor(name, shape, dt))

        def pb(name):
            return ctx.enter_context(nc.psum_tensor(name, [128, 512], f32))

        def sem(name):
            return ctx.enter_context(nc.semaphore(name))

        R = sb("Rraw", [128, NJ, 1024], f32)
        W1S = sb("W1S", [128, 3, 2, 512], f32r)
        W2S = sb("W2S", [128, 3, 2, 512], f32r)
        XT = sb("XT", [128, 2, 2, 4, 512], f32r)
        HS = sb("HS", [128, 3, 2, 512], f32r)
        HF = sb("HF", [128, 2, 512], f32)
        XR = sb("XR", [128, 4, 1024], f32r)
        YH = sb("YH", [128, 4, 512], f32r)
        YL = sb("YL", [128, 4, 512], f32r)
        OB = sb("OB", [128, 4, 512], f32)
        B2 = sb("B2", [128, 2, 512], f32)
        OH = sb("OH", [128, 2, 8, 128], bf16)
        RH = sb("RH", [128, 5, NT, 8], bf16)
        V = sb("V", [128, 5, NT, 8], bf16)
        HM = sb("HM", [128, NT, 8], bf16)
        S = sb("S", [128, NT, E], f32)
        S2 = sb("S2", [128, 256], f32)
        slo = sb("slo", [128, NT, E], i32)
        shi = sb("shi", [128, NT, E], i32)
        ident = sb("ident", [128, 128], f32)
        identr = sb("identr", [128, 128], f32r)
        io128 = sb("io128", [128, 128], f32)
        BO = sb("BO", [128, 128], bf16)
        TRI = sb("TRI", [128, 128], bf16)
        b1 = sb("b1", [128, E * NJ], f32)
        idx = sb("idx", [128, E, 8], u32)
        G = sb("G", [128, E, 8], f32)
        IM = sb("IM", [128, 40], f32)
        idf = sb("idf", [128, 8], f32)
        gs = sb("gs", [128, 8], f32)
        cand = sb("cand", [128, 1], i32)
        mbit = sb("mbit", [128, 1], i32)
        cnt = sb("cnt", [128, 1], bf16)
        r1 = sb("r1", [128, 4], bf16)
        r2 = sb("r2", [128, 4], bf16)
        r3 = sb("r3", [128, 4], bf16)
        offs = sb("offs", [128, 4], f32)
        affb = sb("affb", [128, 4], f32)
        biasc = sb("biasc", [128, 4], f32)
        wr = sb("wr", [128, 4, E], f32)
        wrs = sb("wrs", [128, 4, 2 * E], f32r)
        cT = sb("cT", [128, 2, NB], f32)
        sty = sb("sty", [128, 4, NB], f32)
        sty2 = sb("sty2", [128, 4, NB], f32)
        dv = sb("dv", [128, 4, NB], f32)
        dsq = sb("dsq", [128, 4, NB], f32)
        dr = sb("dr", [128, 4, NB], f32)
        de = sb("de", [128, 4, NB], f32)
        dco = sb("dco", [128, 4, NB], f32)
        mx = sb("mx", [128, 4], f32)
        l0 = sb("l0", [128, 4, E], f32)
        lg = sb("lg", [128, 4, E], f32)
        ex = sb("ex", [128, 4, E], f32)
        sm = sb("sm", [128, 4], f32)
        rs = sb("rs", [128, 4], f32)

        def slot2(s):
            return R[:, s:s + 2, :].rearrange("p s n -> p (s n)").rearrange("p (c n) -> p c n", c=4)

        XB = [slot2(14), slot2(12)]
        YT = [slot2(10), slot2(8)]
        WTraw = slot2(6)
        WSQ = slot2(4)
        AWT = R[:, 2, :].rearrange("p (k n) -> p k n", k=2)
        sg = R[:, 3, 0:256]
        se = R[:, 3, 256:512]
        mg = R[:, 3, 512:768]
        me = R[:, 3, 768:1024]
        sa = R[:, 4, 0:256]
        sbq = R[:, 4, 256:512]
        junk = R[:, 4, 512:768]
        sr = R[:, 5, 0:256]
        sr2 = R[:, 5, 256:512]
        sli = sb("sli", [128, NT * E], i32)
        Jt = sb("Jt", [128, 128], i32)
        Jm = sb("Jm", [128, 128], i32)

        BB = [pb(f"BB{i}") for i in range(4)]
        AB = [pb(f"AB{i}") for i in range(2)]
        TB = pb("TB")
        IB = pb("IB")

        def wt(hl, c):
            return W1S[:, c, hl, :] if c < 3 else W2S[:, 0, hl, :]

        def xbank(n):
            return (TB, AB[0], AB[1], IB)[n % 4] if n < 8 else TB

        def asf(ap):
            return ap.bitcast(f32)

        s_c = {n: sem(f"s_c_{n}") for n in ("aff", "small", "bias", "b1")}
        s_wt = [sem(f"s_wt{c}") for c in range(4)]
        s_x = [sem(f"s_x{i}") for i in range(2)]
        s_id = sem("s_id")
        s_cst = sem("s_cst")
        s_sp = sem("s_sp")
        s_sty = sem("s_sty")
        s_wsq = sem("s_wsq")
        s_dp = sem("s_dp")
        s_dvv = sem("s_dvv")
        s_dsq = sem("s_dsq")
        s_dco = sem("s_dco")
        s_wth = sem("s_wth")
        s_wtl = sem("s_wtl")
        s_xmh = sem("s_xmh")
        s_xml = sem("s_xml")
        s_cp = sem("s_cp")
        s_ce = sem("s_ce")
        s_cl = sem("s_cl")
        s_yh = sem("s_yh")
        s_yl = sem("s_yl")
        s_wr = sem("s_wr")
        s_idr = sem("s_idr")
        s_rt = sem("s_rt")
        s_lg = sem("s_lg")
        s_ex = sem("s_ex")
        s_S = sem("s_S")
        s_yt = sem("s_yt")
        s_yra = sem("s_yra")
        s_yrv = sem("s_yrv")
        s_yrw = sem("s_yrw")
        s_yd = [sem(f"s_yd{i}") for i in range(4)]
        s_o0 = sem("s_o0")
        s_s2t = sem("s_s2t")
        s_s2 = sem("s_s2")
        s_cnt = sem("s_cnt")
        s_pc = sem("s_pc")
        s_rr = sem("s_rr")
        s_off = sem("s_off")
        s_slot = sem("s_slot")
        s_slt = sem("s_slt")
        s_sli = sem("s_sli")
        s_V = sem("s_V")
        s_v = sem("s_v")
        s_p = sem("s_p")
        s_R = sem("s_R")
        s_oh = sem("s_oh")
        s_im = sem("s_im")
        s_imc = sem("s_imc")
        s_idx = sem("s_idx")
        s_raw = [sem(f"s_raw{j}") for j in range(NJ)]
        s_w1h = sem("s_w1h")
        s_w1l = sem("s_w1l")
        s_w2h = sem("s_w2h")
        s_w2l = sem("s_w2l")
        s_A = sem("s_A")
        s_B = sem("s_B")
        s_Bt = sem("s_Bt")
        s_g = sem("s_g")
        s_hl = sem("s_hl")
        s_ev = sem("s_ev")
        s_ob = sem("s_ob")
        s_sc = sem("s_sc")
        s_gat = [sem(f"s_gat{i}") for i in range(4)]
        s_T = sem("s_T")
        s_xh = sem("s_xh")
        s_xl = sem("s_xl")
        s_b2 = [sem(f"s_b2{i}") for i in range(2)]

        block = ctx.enter_context(nc.Block())

        @block.sync
        def _(eng):
            eng.dma_start(AWT, affWT).then_inc(s_c["aff"], 16)
            eng.dma_start(cT[:, :, :], condT).then_inc(s_c["aff"], 16)
            eng.dma_start(affb[:, :], affbT).then_inc(s_c["aff"], 16)
            for c in range(4):
                eng.dma_start(WTraw[:, c, :], WT[:, c, :]).then_inc(s_wt[c], 16)
            eng.dma_start(XB[1], xT[1]).then_inc(s_x[1], 16)
            eng.dma_start(biasc[:, :], biasT).then_inc(s_c["bias"], 16)
            eng.dma_start(wr[:, :, :], WrT).then_inc(s_c["small"], 16)
            eng.dma_start(b1[:, :], b1T).then_inc(s_c["b1"], 16)

            def load_w(e, j):
                eng.dma_start(R[:, j, 0:512], W1[e, j]).then_inc(s_raw[j], 16)
                eng.dma_start(R[:, j, 512:1024], W2[e, j]).then_inc(s_raw[j], 16)

            def load_b2(e):
                eng.dma_start(B2[:, e % 2, :], b2[e:e + 1, :].broadcast_to([128, 512])).then_inc(s_b2[e % 2], 16)

            load_w(0, 0)
            load_w(0, 1)
            load_b2(0)
            load_b2(1)

            def store_rows(b):
                for t in range(4 * b, 4 * b + 4):
                    eng.wait_ge(s_yra, t + 1)
                    if t < NT - 4:
                        eng.wait_ge(s_yrv, t + 1)
                    else:
                        eng.wait_ge(s_yrw, t - (NT - 4) + 1)
                    eng.dma_start(y_d[128 * t:128 * t + 128, :], asf(XR[:, t % 4, :])).then_inc(s_yd[t % 4], 16)

            for b in range(2, NB):
                eng.wait_ge(s_xmh, 4 * (b - 1))
                eng.wait_ge(s_xml, 4 * (b - 1))
                eng.dma_start(XB[b % 2], xT[b]).then_inc(s_x[b % 2], 16)
                if b >= 3:
                    store_rows(b - 3)
            for b in range(NB - 3, NB - 1):
                store_rows(b)
            eng.wait_ge(s_yh, 4 * NB)
            eng.wait_ge(s_yl, 4 * NB)
            for j in [2] + list(range(6, NJ)):
                load_w(0, j)
                if j == 8:
                    store_rows(NB - 1)
            eng.wait_ge(s_slt, 1)
            eng.wait_ge(s_V, 1)
            for j in range(3, 6):
                load_w(0, j)
            for e in range(1, E):
                for j in range(NJ):
                    eng.wait_ge(s_w2h, 32 * (e - 1) + 16 + j + 1)
                    eng.wait_ge(s_w2l, 32 * (e - 1) + 16 + j + 1)
                    load_w(e, j)
                    if e >= 2 and j == 4:
                        eng.wait_ge(s_ev, 8 * (e - 1))
                        load_b2(e)
            for i in range(4):
                eng.wait_ge(s_yd[i], 16 * 8)
            eng.wait_ge(s_sc, 64 * NU)

        @block.gpsimd
        def _(eng):
            eng.memset(ident[:, :], 0.0).then_inc(s_p, 1)
            eng.wait_ge(s_p, 1)
            eng.affine_select(out=ident[:, :], in_=ident[:, :], compare_op=ALU.not_equal, fill=1.0,
                              base=0, pattern=[[-1, 128]], channel_multiplier=1).then_inc(s_id, 1)
            eng.iota(io128[:, :], pattern=[[1, 128]], base=0, channel_multiplier=0,
                     allow_small_or_imprecise_dtypes=True).then_inc(s_cst, 1)
            eng.iota(Jt[:, :], pattern=[[1, 128]], base=128, channel_multiplier=-1).then_inc(s_cst, 1)
            eng.iota(V[:, 0, :, :], pattern=[[0, 256]], base=0, channel_multiplier=1,
                     allow_small_or_imprecise_dtypes=True).then_inc(s_cst, 1)
            eng.iota(V[:, 1, :, :], pattern=[[1, NT], [0, 8]], base=0, channel_multiplier=0,
                     allow_small_or_imprecise_dtypes=True).then_inc(s_cst, 1)
            Sf = S[:, :, :].rearrange("p t e -> p (t e)")
            Vf = [V[:, i, :, :].rearrange("p t e -> p (t e)") for i in range(5)]
            eng.wait_ge(s_S, NB)
            eng.wait_ge(s_wsq, 1)
            eng.wait_ge(s_dp, 1)
            eng.tensor_copy(Vf[2], Sf).then_inc(s_p, 1)
            eng.wait_ge(s_p, 2)
            eng.tensor_tensor(sr, Sf, Vf[2], ALU.subtract).then_inc(s_p, 1)
            eng.wait_ge(s_p, 3)
            eng.tensor_copy(Vf[3], sr).then_inc(s_p, 1)
            eng.wait_ge(s_p, 4)
            eng.tensor_tensor(sr2, sr, Vf[3], ALU.subtract).then_inc(s_p, 1)
            eng.wait_ge(s_p, 5)
            eng.tensor_copy(Vf[4], sr2).then_inc(s_V, 1)

            def gather(u):
                eng.wait_ge(s_idx, u // 2 + 1)
                for t in range(4):
                    c = 4 * (u % 2) + t
                    if u:
                        eng.wait_ge(s_T, 8 * (u - 1) + 2 * t + 2)
                    eng.indirect_dma_start(
                        asf(XR[:, t, :]), None, y_d[:, :],
                        bass.IndirectOffsetOnAxis(idx[:, u // 2, c:c + 1], 0),
                        bounds_check=NT * 128 - 1, oob_is_err=True).then_inc(s_gat[t], 16)

            def scatter(u):
                if u == 0:
                    eng.wait_ge(s_o0, 16)
                else:
                    eng.wait_ge(s_sc, 64 * u)
                for t in range(4):
                    c = 4 * (u % 2) + t
                    eng.wait_ge(s_ob, 4 * u + t + 1)
                    eng.indirect_dma_start(
                        out[:, :], bass.IndirectOffsetOnAxis(idx[:, u // 2, c:c + 1], 0),
                        OB[:, t, :], None,
                        bounds_check=NT * 128 - 1, oob_is_err=True,
                        compute_op=ALU.add).then_inc(s_sc, 16)

            for i in range(4):
                eng.wait_ge(s_yd[i], 16 * 8)
            gather(0)
            gather(1)
            eng.dma_start(out.rearrange("(a b) d -> a (b d)", a=512),
                          x.rearrange("(a b) d -> a (b d)", a=512)).then_inc(s_o0, 16)
            for u in range(NU):
                scatter(u)
                if u + 2 < NU:
                    gather(u + 2)

        @block.scalar
        def _(eng):
            eng.dma_start(XB[0], xT[0]).then_inc(s_x[0], 16)
            for c in range(4):
                eng.wait_ge(s_wt[c], 16)
                eng.activation(wt(0, c), WTraw[:, c, :], ACT.Copy).then_inc(s_wth, 1)
            eng.wait_ge(s_sty, 1)

            def xm_hi(b):
                eng.wait_ge(s_x[b % 2], 16 * (b // 2 + 1))
                if b >= 2:
                    eng.wait_ge(s_cp, 4 * (b - 1))
                for c in range(4):
                    eng.activation(XT[:, b % 2, 0, c, :], XB[b % 2][:, c, :], ACT.Copy,
                                   scale=sty[:, c, b:b + 1]).then_inc(s_xmh, 1)

            def evac(b, o):
                eng.wait_ge(s_cp, 4 * b + o + 1)
                if b >= 2:
                    eng.wait_ge(s_yl, 4 * (b - 1))
                eng.activation(YT[b % 2][:, o, :], BB[o][:, :], ACT.Identity,
                               scale=dco[:, o, b:b + 1], bias=biasc[:, o:o + 1]).then_inc(s_ce, 1)

            def y_hi(b):
                if b:
                    eng.wait_ge(s_yt, 8 * b)
                    eng.wait_ge(s_rt, b)
                for c in range(4):
                    eng.wait_ge(s_cl, 4 * b + c + 1)
                    eng.activation(YH[:, c, :], YT[b % 2][:, c, :], ACT.Copy).then_inc(s_yh, 1)

            def exps(b):
                eng.wait_ge(s_lg, b + 1)
                eng.activation(ex[:, :, :], lg[:, :, :], ACT.Exp).then_inc(s_ex, 1)

            def row_hi(t):
                eng.wait_ge(s_yt, 2 * t + 1)
                if t >= 4:
                    eng.wait_ge(s_yd[t % 4], 16 * (t // 4))
                eng.activation(XR[:, t % 4, 0:512], TB[:, :], ACT.Copy).then_inc(s_yra, 1)

            xm_hi(0)
            eng.activation(WSQ, WTraw, ACT.Square).then_inc(s_wsq, 1)
            xm_hi(1)
            eng.wait_ge(s_dvv, 1)
            eng.activation(dsq[:, :, :], dv[:, :, :], ACT.Sqrt).then_inc(s_dsq, 1)
            eng.wait_ge(s_c["small"], 16)
            eng.activation(wrs[:, :, 0:E], wr[:, :, :], ACT.Copy).then_inc(s_wr, 1)
            eng.wait_ge(s_id, 1)
            eng.activation(identr[:, :], ident[:, :], ACT.Copy).then_inc(s_idr, 1)
            eng.wait_ge(s_dco, 1)
            eng.wait_ge(s_c["bias"], 16)
            for b in range(NB):
                evac(b, 0)
                evac(b, 1)
                if b:
                    exps(b - 1)
                    row_hi(4 * b - 4)
                    row_hi(4 * b - 3)
                evac(b, 2)
                if b:
                    row_hi(4 * b - 2)
                evac(b, 3)
                if b:
                    row_hi(4 * b - 1)
                y_hi(b)
                if b + 2 < NB:
                    xm_hi(b + 2)
            exps(NB - 1)
            for t in range(NT - 4, NT):
                row_hi(t)
                eng.wait_ge(s_yt, 2 * t + 2)
                eng.activation(XR[:, t % 4, 512:1024], IB[:, :], ACT.Copy).then_inc(s_yrw, 1)

            def w1_hi(i):
                j = i % NJ
                eng.wait_ge(s_raw[j], 32 * (i // 32 + 1))
                if i >= 3:
                    eng.wait_ge(s_A, i - 2)
                elif i < 3:
                    eng.wait_ge(s_cp, 4 * NB)
                eng.activation(W1S[:, i % 3, 0, :], R[:, j, 0:512], ACT.Copy).then_inc(s_w1h, 1)

            def w2_hi(i):
                j = i % NJ
                eng.wait_ge(s_raw[j], 32 * (i // 32 + 1))
                if i >= 3:
                    eng.wait_ge(s_B, i - 2)
                eng.activation(W2S[:, i % 3, 0, :], R[:, j, 512:1024], ACT.Copy).then_inc(s_w2h, 1)

            def x_hi(u, t):
                n = 8 * u + 2 * t
                eng.wait_ge(s_T, n + 1)
                eng.activation(XT[:, u % 2, 0, :, 128 * t:128 * t + 128],
                               xbank(n)[:, :].rearrange("p (c n) -> p c n", c=4), ACT.Copy).then_inc(s_xh, 1)

            w1_hi(0)
            w1_hi(1)
            for t in range(4):
                x_hi(0, t)
            for i in range(NBLK):
                if i + 2 < NBLK:
                    w1_hi(i + 2)
                w2_hi(i)
                eng.wait_ge(s_A, i + 1)
                if i >= 2:
                    eng.wait_ge(s_hl, i - 1)
                bias = b1[:, (i // 32) * NJ + i % NJ:(i // 32) * NJ + i % NJ + 1]
                if i == 0:
                    eng.wait_ge(s_c["b1"], 16)
                eng.activation(HF[:, i % 2, :], AB[i % 2][:, :], ACT.Gelu, bias=bias)
                eng.activation(HS[:, i % 3, 0, :], AB[i % 2][:, :], ACT.Gelu, bias=bias).then_inc(s_g, 1)
                u, j = i // NJ, i % NJ
                if u + 1 < NU and j in (5, 7, 9, 11):
                    x_hi(u + 1, (j - 5) // 2)

        @block.vector
        def _(eng):
            chain = [0]

            def link(ins):
                chain[0] += 1
                ins.then_inc(s_v, 1)
                eng.wait_ge(s_v, chain[0])

            eng.wait_ge(s_c["aff"], 48)
            eng.wait_ge(s_sp, 1)
            link(eng.scalar_tensor_tensor(sty[:, :, :], IB[:, 0:32].rearrange("p (c b) -> p c b", c=4), 1.0 / 16.0,
                                          affb[:, :, None].broadcast_to([128, 4, NB]), ALU.mult, ALU.add))
            eng.tensor_tensor(sty2[:, :, :], sty[:, :, :], sty[:, :, :], ALU.mult).then_inc(s_sty, 1)
            for c in range(4):
                eng.wait_ge(s_wt[c], 16)
                eng.wait_ge(s_wth, c + 1)
                eng.tensor_tensor(wt(1, c), WTraw[:, c, :], asf(wt(0, c)), ALU.subtract).then_inc(s_wtl, 1)

            def xm_lo(b):
                eng.wait_ge(s_x[b % 2], 16 * (b // 2 + 1))
                for c in range(4):
                    eng.wait_ge(s_xmh, 4 * b + c + 1)
                    eng.scalar_tensor_tensor(XT[:, b % 2, 1, c, :], XB[b % 2][:, c, :], sty[:, c, b:b + 1],
                                             asf(XT[:, b % 2, 0, c, :]), ALU.mult, ALU.subtract).then_inc(s_xml, 1)

            xm_lo(0)
            eng.wait_ge(s_dp, 1)
            eng.tensor_scalar(dv[:, :, :], TB[:, 0:32].rearrange("p (c b) -> p c b", c=4), 1e-8, None,
                              ALU.add).then_inc(s_dvv, 1)
            xm_lo(1)
            eng.wait_ge(s_dsq, 1)
            link(eng.reciprocal(dr[:, :, :], dsq[:, :, :]))
            link(eng.tensor_tensor(de[:, :, :], dv[:, :, :], dr[:, :, :], ALU.mult))
            link(eng.tensor_tensor(de[:, :, :], de[:, :, :], dr[:, :, :], ALU.mult))
            link(eng.tensor_scalar(de[:, :, :], de[:, :, :], -0.5, 1.5, ALU.mult, ALU.add))
            eng.tensor_tensor(dco[:, :, :], dr[:, :, :], de[:, :, :], ALU.mult).then_inc(s_dco, 1)
            eng.wait_ge(s_cst, 4)
            link(eng.tensor_scalar(Jm[:, :], Jt[:, :], 7, None, ALU.bitwise_and))
            link(eng.tensor_scalar(BO[:, :], Jm[:, :], 0.0, None, ALU.is_equal))
            link(eng.scalar_tensor_tensor(TRI[:, :], Jt[:, :], 128.0, BO[:, :], ALU.is_gt, ALU.mult))

            eng.wait_ge(s_wr, 1)
            eng.tensor_tensor(wrs[:, :, E:2 * E], wr[:, :, :], asf(wrs[:, :, 0:E]), ALU.subtract).then_inc(s_wr, 1)

            def clip(b, o):
                eng.wait_ge(s_ce, 4 * b + o + 1)
                yv = YT[b % 2][:, o, :]
                eng.tensor_scalar(yv, yv, -CLAMP, CLAMP, ALU.max, ALU.min).then_inc(s_cl, 1)

            def y_lo(b):
                if b:
                    eng.wait_ge(s_yt, 8 * b)
                    eng.wait_ge(s_rt, b)
                for c in range(4):
                    eng.wait_ge(s_yh, 4 * b + c + 1)
                    eng.tensor_tensor(YL[:, c, :], YT[b % 2][:, c, :], asf(YH[:, c, :]),
                                      ALU.subtract).then_inc(s_yl, 1)

            def row_lo(t):
                eng.wait_ge(s_yt, 2 * t + 2)
                if t >= 4:
                    eng.wait_ge(s_yd[t % 4], 16 * (t // 4))
                eng.tensor_copy(XR[:, t % 4, 512:1024], IB[:, :]).then_inc(s_yrv, 1)

            def softmax_head(q):
                eng.wait_ge(s_rt, q + 1)
                L = AB[q % 2][:, 0:64].rearrange("p (t k e) -> p t e k", t=4, k=2)
                link(eng.tensor_reduce(l0[:, :, :], L, AX.X, ALU.add))
                link(eng.tensor_reduce(mx[:, :], l0[:, :, :], AX.X, ALU.max))
                if q:
                    eng.wait_ge(s_ex, q)
                eng.tensor_tensor(lg[:, :, :], l0[:, :, :], mx[:, :, None].broadcast_to([128, 4, E]),
                                  ALU.subtract).then_inc(s_lg, 1)

            def softmax_tail(q):
                eng.wait_ge(s_ex, q + 1)
                link(eng.tensor_reduce(sm[:, :], ex[:, :, :], AX.X, ALU.add))
                link(eng.reciprocal(rs[:, :], sm[:, :]))
                eng.tensor_tensor(S[:, 4 * q:4 * q + 4, :], ex[:, :, :],
                                  rs[:, :, None].broadcast_to([128, 4, E]), ALU.mult).then_inc(s_S, 1)

            for b in range(NB):
                clip(b, 0)
                clip(b, 1)
                if b:
                    softmax_head(b - 1)
                    row_lo(4 * b - 4)
                    softmax_tail(b - 1)
                    row_lo(4 * b - 3)
                clip(b, 2)
                if b:
                    row_lo(4 * b - 2)
                clip(b, 3)
                if b:
                    row_lo(4 * b - 1)
                y_lo(b)
                if b + 2 < NB:
                    xm_lo(b + 2)
            softmax_head(NB - 1)
            softmax_tail(NB - 1)

            eng.memset(cand[:, :], 1 << 29)
            eng.wait_ge(s_s2t, 1)
            link(eng.tensor_copy(S2[:, :], AB[0][:, 0:256]))
            for n, bit in enumerate(range(29, -1, -1)):
                eng.tensor_scalar(junk, S2[:, :], cand[:, :].bitcast(f32), None, ALU.is_ge, ALU.add,
                                  accum_out=cnt[:, :]).then_inc(s_cnt, 1)
                eng.wait_ge(s_pc, n + 1)
                link(eng.tensor_scalar(mbit[:, :], AB[1][:, 0:1], float(K), float(1 << bit), ALU.is_lt, ALU.mult))
                half = (1 << (bit - 1)) if bit else 0
                link(eng.scalar_tensor_tensor(cand[:, :], mbit[:, :], half, cand[:, :],
                                              ALU.bitwise_or, ALU.bitwise_xor))
            thr = cand[:, :].bitcast(f32)
            eng.tensor_scalar(mg, S2[:, :], thr, None, ALU.is_gt)
            link(eng.tensor_scalar(me, S2[:, :], thr, None, ALU.is_equal))
            for h in range(2):
                q = slice(128 * h, 128 * h + 128)
                eng.tensor_tensor_scan(sg[:, q], mg[:, q], mg[:, q], 0.0, ALU.add, ALU.max)
                last = eng.tensor_tensor_scan(se[:, q], me[:, q], me[:, q], 0.0, ALU.add, ALU.max)
            link(last)
            eng.memset(r2[:, :], 0.0)
            eng.memset(r3[:, :], 0.0)
            eng.tensor_copy(r1[:, 0:2], sg[:, 127:256:128])
            link(eng.tensor_copy(r1[:, 2:4], se[:, 127:256:128]))
            eng.tensor_copy(r2[:, 1:4:2], r1[:, 0:4:2])
            link(eng.tensor_tensor(r3[:, 2:3], r1[:, 0:1], r1[:, 1:2], ALU.add))
            eng.tensor_copy(r3[:, 3:4], r3[:, 2:3]).then_inc(s_rr, 1)
            eng.wait_ge(s_off, 1)
            link(eng.tensor_copy(offs[:, :], AB[1][:, 0:4]))
            for h in range(2):
                q = slice(128 * h, 128 * h + 128)
                eng.scalar_tensor_tensor(sa[:, q], sg[:, q], offs[:, h:h + 1], mg[:, q], ALU.add, ALU.mult)
                last = eng.scalar_tensor_tensor(sbq[:, q], se[:, q], offs[:, 2 + h:3 + h], me[:, q], ALU.add, ALU.mult)
            link(last)
            eng.tensor_tensor(sa, sa, sbq, ALU.add).then_inc(s_slot, 1)
            eng.wait_ge(s_slt, 1)
            link(eng.tensor_scalar(sli[:, :], AB[0][:, 0:256], -1.0, None, ALU.add))
            eng.tensor_scalar(slo[:, :, :].rearrange("p t e -> p (t e)"), sli[:, :], 127, None, ALU.bitwise_and)
            link(eng.tensor_scalar(shi[:, :, :].rearrange("p t e -> p (t e)"), sli[:, :], 7, None,
                                   ALU.arith_shift_right))
            eng.wait_ge(s_V, 1)

            def build_rhs(e):
                if e:
                    eng.wait_ge(s_im, 4 * e)
                link(eng.tensor_tensor(HM[:, :, :], shi[:, :, e:e + 1].broadcast_to([128, NT, 8]),
                                       io128[:, None, 0:8].broadcast_to([128, NT, 8]), ALU.is_equal))
                eng.tensor_tensor(RH[:, :, :, :], V[:, :, :, e:e + 1].broadcast_to([128, 5, NT, 8]),
                                  HM[:, None, :, :].broadcast_to([128, 5, NT, 8]), ALU.mult).then_inc(s_R, 1)

            def build_oh(e, q):
                n = 4 * e + q
                if n >= 2:
                    eng.wait_ge(s_im, n - 1)
                eng.tensor_tensor(OH[:, n % 2, :, :],
                                  slo[:, 8 * q:8 * q + 8, e:e + 1].broadcast_to([128, 8, 128]),
                                  io128[:, None, :].broadcast_to([128, 8, 128]), ALU.is_equal).then_inc(s_oh, 1)

            def finish_idx(e):
                eng.wait_ge(s_im, 4 * e + 4)
                eng.tensor_copy(IM[:, :], IB[:, 0:40]).then_inc(s_imc, 1)
                eng.wait_ge(s_imc, e + 1)
                link(eng.scalar_tensor_tensor(idf[:, :], IM[:, 8:16], 128.0, IM[:, 0:8], ALU.mult, ALU.add))
                eng.tensor_tensor(gs[:, :], IM[:, 16:24], IM[:, 24:32], ALU.add)
                link(eng.tensor_copy(idx[:, e, :], idf[:, :]))
                eng.tensor_tensor(G[:, e, :], gs[:, :], IM[:, 32:40], ALU.add).then_inc(s_idx, 1)

            build_rhs(0)
            for q in range(4):
                build_oh(0, q)
            finish_idx(0)

            def w1_lo(i):
                eng.wait_ge(s_w1h, i + 1)
                eng.tensor_tensor(W1S[:, i % 3, 1, :], R[:, i % NJ, 0:512], asf(W1S[:, i % 3, 0, :]),
                                  ALU.subtract).then_inc(s_w1l, 1)

            def w2_lo(i):
                eng.wait_ge(s_w2h, i + 1)
                eng.tensor_tensor(W2S[:, i % 3, 1, :], R[:, i % NJ, 512:1024], asf(W2S[:, i % 3, 0, :]),
                                  ALU.subtract).then_inc(s_w2l, 1)

            def x_lo(u, t):
                n = 8 * u + 2 * t + 1
                eng.wait_ge(s_T, n + 1)
                eng.tensor_copy(XT[:, u % 2, 1, :, 128 * t:128 * t + 128],
                                xbank(n)[:, :].rearrange("p (c n) -> p c n", c=4)).then_inc(s_xl, 1)

            def evac_add(u):
                e = u // 2
                eng.wait_ge(s_b2[e % 2], 16 * (e // 2 + 1))
                if u:
                    eng.wait_ge(s_sc, 64 * u)
                for t in range(4):
                    eng.wait_ge(s_Bt, 4 * u + t + 1)
                    eng.tensor_tensor(OB[:, t, :], BB[t][:, :], B2[:, e % 2, :], ALU.add).then_inc(s_ev, 1)

            def evac_mul(u):
                e = u // 2
                for t in range(4):
                    c = 4 * (u % 2) + t
                    eng.wait_ge(s_ev, 4 * u + t + 1)
                    eng.tensor_scalar(OB[:, t, :], OB[:, t, :], G[:, e, c:c + 1], None, ALU.mult).then_inc(s_ob, 1)

            w1_lo(0)
            w1_lo(1)
            for t in range(4):
                x_lo(0, t)
            for i in range(NBLK + 2):
                if i + 2 < NBLK:
                    w1_lo(i + 2)
                if i < NBLK:
                    w2_lo(i)
                    eng.wait_ge(s_g, i + 1)
                    eng.tensor_tensor(HS[:, i % 3, 1, :], HF[:, i % 2, :], asf(HS[:, i % 3, 0, :]),
                                      ALU.subtract).then_inc(s_hl, 1)
                u, j = i // NJ, i % NJ
                if u >= 1 and j == 1:
                    evac_add(u - 1)
                if u >= 1 and j == 2 and i < NBLK:
                    evac_mul(u - 1)
                if i == NBLK + 1:
                    evac_mul(NU - 1)
                if u + 1 < NU and j in (6, 8, 10, 12):
                    x_lo(u + 1, (j - 6) // 2)
                if u % 2 == 0 and u + 2 < NU:
                    e = u // 2 + 1
                    if j == 3:
                        build_rhs(e)
                    if j in (3, 5, 7, 9):
                        build_oh(e, (j - 3) // 2)
                    if j == 13:
                        finish_idx(e)

        @block.tensor
        def _(eng):
            mm = nc.tensor.matmul
            eng.wait_ge(s_c["aff"], 48)
            for c in range(4):
                for k in range(2):
                    last = mm(IB[:, 8 * c:8 * c + 8], AWT[:, k, 128 * c:128 * c + 128], cT[:, k, :],
                              start=(k == 0), stop=(k == 1))
            last.then_inc(s_sp, 1)

            def demod():
                eng.wait_ge(s_sty, 1)
                eng.wait_ge(s_wsq, 1)
                for o in range(4):
                    for c in range(4):
                        last = mm(TB[:, 8 * o:8 * o + 8], WSQ[:, c, 128 * o:128 * o + 128], sty2[:, c, :],
                                  start=(c == 0), stop=(c == 3))
                last.then_inc(s_dp, 1)

            def cond(b, o, cs):
                if b and cs[0] == 0:
                    eng.wait_ge(s_ce, 4 * (b - 1) + o + 1)
                for c in cs:
                    if o == 0:
                        eng.wait_ge(s_xmh, 4 * b + c + 1)
                        eng.wait_ge(s_xml, 4 * b + c + 1)
                        if b == 0:
                            eng.wait_ge(s_wth, c + 1)
                            eng.wait_ge(s_wtl, c + 1)
                    for n, (a, d) in enumerate(((0, 0), (0, 1), (1, 0))):
                        last = mm(BB[o][:, :], wt(a, c)[:, 128 * o:128 * o + 128], XT[:, b % 2, d, c, :],
                                  start=(c == 0 and n == 0), stop=(c == 3 and n == 2))
                if cs[-1] == 3:
                    last.then_inc(s_cp, 1)

            def router(b):
                eng.wait_ge(s_yh, 4 * b + 4)
                eng.wait_ge(s_yl, 4 * b + 4)
                if b == 0:
                    eng.wait_ge(s_wr, 2)
                if b >= 2:
                    eng.wait_ge(s_lg, b - 1)
                for t in range(4):
                    for c in range(4):
                        for n, Y in enumerate((YH, YL)):
                            last = mm(AB[b % 2][:, 16 * t:16 * t + 16], Y[:, c, 128 * t:128 * t + 128],
                                      wrs[:, c, :], start=(c == 0 and n == 0), stop=(c == 3 and n == 1))
                last.then_inc(s_rt, 1)

            def rows(t):
                if t == 0:
                    eng.wait_ge(s_idr, 1)
                    eng.wait_ge(s_dvv, 1)
                q = slice(128 * (t % 4), 128 * (t % 4) + 128)
                for Y, bank in ((YH, TB), (YL, IB)):
                    if t:
                        if Y is YH:
                            eng.wait_ge(s_yra, t)
                        elif t <= NT - 4:
                            eng.wait_ge(s_yrv, t)
                        else:
                            eng.wait_ge(s_yrw, t - (NT - 4))
                    for c in range(4):
                        last = mm(bank[:, 128 * c:128 * c + 128], Y[:, c, q], identr[:, :], start=True, stop=True)
                    last.then_inc(s_yt, 1)

            for b in range(NB):
                cond(b, 0, (0, 1, 2, 3))
                cond(b, 1, (0, 1, 2, 3))
                if b == 0:
                    demod()
                else:
                    router(b - 1)
                    rows(4 * b - 4)
                cond(b, 2, (0, 1))
                if b:
                    rows(4 * b - 3)
                cond(b, 2, (2, 3))
                cond(b, 3, (0, 1))
                if b:
                    rows(4 * b - 2)
                cond(b, 3, (2, 3))
                if b:
                    rows(4 * b - 1)
            router(NB - 1)
            eng.wait_ge(s_S, NB)
            for h in range(2):
                last = nc.tensor.transpose(AB[0][:, 128 * h:128 * h + 128],
                                           S[:, 16 * h:16 * h + 16, :].rearrange("p t e -> p (t e)"), ident[:, :])
            last.then_inc(s_s2t, 1)
            for n in range(30):
                eng.wait_ge(s_cnt, n + 1)
                mm(AB[1][:, 0:1], BO[:, :], cnt[:, :], start=True, stop=True).then_inc(s_pc, 1)
                if 1 <= n <= 4:
                    rows(NT - 5 + n)
            eng.wait_ge(s_rr, 1)
            mm(AB[1][:, 0:4], TRI[:, :], r1[:, :], start=True, stop=False)
            mm(AB[1][:, 0:4], BO[:, :], r2[:, :], start=False, stop=False)
            mm(AB[1][:, 0:4], BO[:, :], r3[:, :], start=False, stop=True).then_inc(s_off, 1)
            eng.wait_ge(s_slot, 1)
            for h in range(2):
                last = nc.tensor.transpose(AB[0][:, 128 * h:128 * h + 128], sa[:, 128 * h:128 * h + 128], ident[:, :])
            last.then_inc(s_slt, 1)

            def lists(e, q):
                if q == 0:
                    eng.wait_ge(s_R, e + 1)
                    if e:
                        eng.wait_ge(s_imc, e)
                    else:
                        eng.wait_ge(s_yrw, 4)
                eng.wait_ge(s_oh, 4 * e + q + 1)
                for k in range(8):
                    t = 8 * q + k
                    last = mm(IB[:, 0:40].rearrange("p (v h) -> p v h", v=5), OH[:, (4 * e + q) % 2, k, :],
                              RH[:, :, t, :], start=(t == 0), stop=(t == NT - 1))
                last.then_inc(s_im, 1)

            def x_transpose(u, r):
                n = 8 * u + r
                t = r // 2
                if r % 2 == 0:
                    eng.wait_ge(s_gat[t], 16 * (u + 1))
                if n >= 8:
                    if n % 2:
                        eng.wait_ge(s_xh, (n + 1) // 2)
                    else:
                        eng.wait_ge(s_xl, n // 2)
                elif n >= 4:
                    eng.wait_ge(s_xl if n % 2 else s_xh, (n - 4) // 2 + 1)
                elif n == 0:
                    eng.wait_ge(s_yra, NT)
                elif n == 3:
                    eng.wait_ge(s_imc, 1)
                bank = xbank(n)
                for c in range(4):
                    col = 512 * (r % 2) + 128 * c
                    last = mm(bank[:, 128 * c:128 * c + 128], XR[:, t, col:col + 128], identr[:, :],
                              start=True, stop=True)
                last.then_inc(s_T, 1)

            def A(i):
                u = i // NJ
                if i % NJ == 0:
                    eng.wait_ge(s_xh, 4 * u + 4)
                    eng.wait_ge(s_xl, 4 * u + 4)
                if i >= 2:
                    eng.wait_ge(s_g, i - 1)
                eng.wait_ge(s_w1h, i + 1)
                eng.wait_ge(s_w1l, i + 1)
                for c in range(4):
                    for n, (a, d) in enumerate(((0, 0), (0, 1), (1, 0))):
                        last = mm(AB[i % 2][:, :], W1S[:, i % 3, a, 128 * c:128 * c + 128], XT[:, u % 2, d, c, :],
                                  start=(c == 0 and n == 0), stop=(c == 3 and n == 2))
                last.then_inc(s_A, 1)

            def B(i):
                u, j = i // NJ, i % NJ
                eng.wait_ge(s_w2h, i + 1)
                eng.wait_ge(s_w2l, i + 1)
                eng.wait_ge(s_g, i + 1)
                eng.wait_ge(s_hl, i + 1)
                for t in range(4):
                    if j == 0 and u:
                        eng.wait_ge(s_ev, 4 * (u - 1) + t + 1)
                    for n, (a, d) in enumerate(((0, 0), (0, 1), (1, 0))):
                        last = mm(BB[t][:, :], HS[:, i % 3, a, 128 * t:128 * t + 128], W2S[:, i % 3, d, :],
                                  start=(j == 0 and n == 0), stop=(j == NJ - 1 and n == 2))
                    if j == NJ - 1:
                        last.then_inc(s_Bt, 1)
                if j == NJ - 1:
                    eng.wait_ge(s_Bt, 4 * u + 4)
                    eng.sem_inc(s_B, 1)
                else:
                    last.then_inc(s_B, 1)

            for q in range(4):
                lists(0, q)
            for r in range(8):
                x_transpose(0, r)
            for i in range(NBLK + 2):
                if i < NBLK:
                    A(i)
                u, j = i // NJ, i % NJ
                if u + 1 < NU and 5 <= j <= 12:
                    x_transpose(u + 1, j - 5)
                if u % 2 == 0 and u + 2 < NU and j in (5, 7, 9, 11):
                    lists(u // 2 + 1, (j - 5) // 2)
                if i >= 2:
                    B(i - 2)


_OUT = (8, 512, 512)


def kernel(x, cond_512, L0_cond_weight, L0_cond_bias, L0_cond_affine_w, L0_cond_affine_b, L0_ffn_Wr,
           L0_ffn_W1, L0_ffn_b1, L0_ffn_W2, L0_ffn_b2):
    import numpy as np
    import concourse.bacc as bacc
    from concourse import mybir
    from concourse.bass_utils import run_bass_kernel_spmd

    def chunks(a, n):
        a = np.asarray(a)
        return np.ascontiguousarray(a.reshape(n, 128, -1).transpose(1, 0, 2))

    x = np.asarray(x)
    arrays = {
        "xT": np.ascontiguousarray(x.reshape(8, 512, 4, 128).transpose(0, 3, 2, 1)),
        "x": np.ascontiguousarray(x.reshape(4096, 512)),
        "condT": chunks(np.asarray(cond_512).T, 2),
        "WT": chunks(np.asarray(L0_cond_weight).T, 4),
        "biasT": np.ascontiguousarray(np.asarray(L0_cond_bias).reshape(4, 128).T),
        "affWT": chunks(np.asarray(L0_cond_affine_w).T, 2),
        "affbT": np.ascontiguousarray(np.asarray(L0_cond_affine_b).reshape(4, 128).T),
        "WrT": chunks(L0_ffn_Wr, 4),
        "W1": np.ascontiguousarray(
            np.asarray(L0_ffn_W1).reshape(8, 4, 128, 16, 128).transpose(0, 3, 2, 1, 4)).reshape(8, 16, 128, 512),
        "b1T": np.ascontiguousarray(np.asarray(L0_ffn_b1).reshape(8, 16, 128).transpose(2, 0, 1)).reshape(128, 128),
        "W2": np.ascontiguousarray(np.asarray(L0_ffn_W2).reshape(8, 16, 128, 512)),
        "b2": np.ascontiguousarray(np.asarray(L0_ffn_b2)),
    }
    nc = bacc.Bacc("TRN2", target_bir_lowering=False, num_devices=1)
    f32 = mybir.dt.float32
    args = {n: nc.dram_tensor(f"in_{n}", a.shape, f32, kind="ExternalInput").ap() for n, a in arrays.items()}
    out = nc.dram_tensor("out_0", (4096, 512), f32, kind="ExternalOutput").ap()
    adaln_moe_kernel(nc, out=out, **args)
    r = run_bass_kernel_spmd(nc, [{f"in_{n}": a for n, a in arrays.items()}], core_ids=[0])
    return r.results[0]["out_0"].reshape(_OUT)
```

```python
import concourse.bass as bass
from concourse import mybir
from contextlib import ExitStack


def adaln_moe_kernel(nc, xT, x, condT, WT, biasT, affWT, affbT, WrT, W1, b1T, W2, b2, out):
    f32 = mybir.dt.float32
    f32r = mybir.dt.float32r
    bf16 = mybir.dt.bfloat16
    i32 = mybir.dt.int32
    u32 = mybir.dt.uint32
    u16 = mybir.dt.uint16
    ALU = mybir.AluOpType
    ACT = mybir.ActivationFunctionType
    AX = mybir.AxisListType

    NB = 8
    NT = 32
    E = 8
    K = 1024
    NU = 2 * E
    NJ = 16
    NBLK = NU * NJ
    CLAMP = 256.0

    y_d = nc.dram_tensor("y_rows", (NT * 128, 1024), u16, kind="Internal").ap()

    ctx = ExitStack()
    with ctx:
        def sb(name, shape, dt):
            return ctx.enter_context(nc.sbuf_tensor(name, shape, dt))

        def sem(name):
            return ctx.enter_context(nc.semaphore(name))

        R = sb("Rraw", [128, NJ, 1024], f32)
        W1S = sb("W1S", [128, 3, 2, 512], f32r)
        W2S = sb("W2S", [128, 3, 2, 512], f32r)
        XT = sb("XT", [128, 2, 2, 4, 512], f32r)
        HY = sb("HY", [128, 8, 512], f32r)
        HS = HY[:, 0:6, :].rearrange("p (r h) n -> p r h n", h=2)
        HF = sb("HF", [128, 2, 512], f32)
        XR = sb("XR", [128, 4, 1024], u16)
        XU = sb("XU", [128, 4, 8, 128], u16)
        XF = sb("XF", [128, 2, 512], f32)
        YH = HY[:, 0:4, :]
        YL = HY[:, 4:8, :]
        BG = sb("BG", [128, 512], f32)
        OB = sb("OB", [128, 4, 512], f32)
        B2 = sb("B2", [128, 2, 512], f32)
        OH = sb("OH", [128, 4, 8, 128], bf16)
        RH = sb("RH", [128, 5, NT, 8], bf16)
        V = sb("V", [128, 5, NT, 8], bf16)
        HM = sb("HM", [128, NT, 8], bf16)
        S = sb("S", [128, NT, E], f32)
        S2 = sb("S2", [128, 256], f32)
        slo = sb("slo", [128, NT, E], i32)
        shi = sb("shi", [128, NT, E], i32)
        ident = sb("ident", [128, 128], f32)
        io128 = sb("io128", [128, 128], f32)
        BO = sb("BO", [128, 128], bf16)
        TRI = sb("TRI", [128, 128], bf16)
        b1 = sb("b1", [128, E * NJ], f32)
        idx = sb("idx", [128, E, 8], u32)
        G = sb("G", [128, E, 8], f32)
        cand = sb("cand", [128, 4], i32)
        cnext = sb("cnext", [128, 4, 4], i32)
        cnt = sb("cnt", [128, 3], bf16)
        r1 = sb("r1", [128, 4], bf16)
        affb = sb("affb", [128, 4], f32)
        biasc = sb("biasc", [128, 4], f32)
        wr = sb("wr", [128, 4, E], f32)
        IR = sb("IR", [128, 128], f32r)
        RW = sb("RW", [128, 4, 2 * E], f32r)
        L1 = sb("L1", [2 * E, 512], f32)
        PS = sb("PS", [2 * E, E], f32)
        BOS = sb("BOS", [128, 128], bf16)
        KR = sb("KR", [1, 128], bf16)
        KC = sb("KC", [1, 2], bf16)
        cT = sb("cT", [128, 2, NB], f32)
        sty = sb("sty", [128, 4, NB], f32)
        dco = sb("dco", [128, 4, NB], f32)
        gtab = sb("gtab", [128, 2], f32)
        mx = sb("mx", [128, 4], f32)
        lg = sb("lg", [128, 4, E], f32)
        ex = sb("ex", [128, 4, E], f32)
        sm = sb("sm", [128, 4], f32)
        rs = sb("rs", [128, 4], f32)

        def slot2(s):
            return R[:, s:s + 2, :].rearrange("p s n -> p (s n)").rearrange("p (c n) -> p c n", c=4)

        XB = [slot2(14), slot2(12)]
        YT = [slot2(10), slot2(8)]
        WTraw = slot2(6)
        WSQ = slot2(4)
        AWT = R[:, 2, :].rearrange("p (k n) -> p k n", k=2)
        SC = OB[:, :, :].rearrange("p c n -> p (c n)")
        sg, se, mg, me, junk = (SC[:, 256 * i:256 * i + 256] for i in range(5))
        SQ = SC[:, 0:1024]
        S2h = SC[:, 1280:1408].bitcast(bf16)
        sa = HY[:, 6, 0:256]
        sbq = HY[:, 7, 0:256]
        sr = R[:, 5, 0:256]
        sr2 = R[:, 5, 256:512]
        XW = XF[:, :, :].rearrange("p a n -> p (a n)")
        taken = [0]

        def early(dims, dt):
            n = 1
            for d in dims:
                n *= d
            words = (n + 1) // 2 if dt == bf16 else n
            v = XW[:, taken[0]:taken[0] + words]
            taken[0] += words
            v = v if dt == f32 else v.bitcast(dt)
            v = v[:, 0:n]
            if len(dims) == 2:
                v = v.rearrange("p (a b) -> p a b", a=dims[0])
            return v

        sty2 = early([4, NB], f32)
        dv = early([4, NB], f32)
        dsq = early([4, NB], f32)
        dr = early([4, NB], f32)
        de = early([4, NB], f32)
        Jm = early([128], i32)
        slo0 = early([NT], i32)
        shi0 = early([NT], i32)
        J8 = early([8], i32)
        TT = early([11, 8], i32)
        C0 = early([8], i32)
        CN = early([8, 8], i32)
        ge0 = early([7, NT], bf16)
        cnt0 = early([7], bf16)
        mge = early([2, NT], bf16)
        sc0 = early([2 * NT], f32)
        sw0 = early([2, NT], f32)
        sl0 = early([NT], i32)
        nsl0 = sb("nsl0", [128, NT], f32)
        ON = early([128], bf16)
        OS = early([128], bf16)
        DT = early([128], bf16)
        ones = sb("ones", [1, 128], bf16)
        kmag = sb("kmag", [1, 2, 128], bf16)
        Jt = sb("Jt", [128, 128], i32)

        BBt = ctx.enter_context(nc.psum_tensor("BBt", [128, 4, 512], f32))
        Pt = ctx.enter_context(nc.psum_tensor("Pt", [128, 4, 512], f32))
        BB = [BBt[:, i, :] for i in range(4)]
        TB, IB = Pt[:, 0, :], Pt[:, 1, :]
        AB = [Pt[:, 2, :], Pt[:, 3, :]]

        YP = [R[:, 4:6, :].rearrange("p s n -> p (s n)").bitcast(u16).rearrange("p (t k n) -> p t k n", t=4, k=8),
              XU[:, :, :, :]]

        def planes(b, h, c):
            return YP[b % 2][:, :, 4 * h + c, :]

        def words(b, c):
            return YT[b % 2][:, c, :].bitcast(u16).rearrange("p (t n h) -> p t n h", t=4, h=2)

        def wt(hl, c):
            return W1S[:, c, hl, :] if c < 3 else W2S[:, 0, hl, :]

        def halves(n):
            return XF[:, n % 2, :].bitcast(u16).rearrange("p (n h) -> p n h", h=2)

        def x_block(u, t):
            return (11, 12, 12, 13)[t] if u == 1 else 6 + 2 * t

        def asf(ap):
            return ap.bitcast(f32)

        s_c = {n: sem(f"s_c_{n}") for n in ("aff", "small", "bias", "b1")}
        s_wt = [sem(f"s_wt{c}") for c in range(4)]
        s_x0 = [sem(f"s_x0{c}") for c in range(4)]
        s_x = [sem(f"s_x{i}") for i in range(2)]
        s_id = sem("s_id")
        s_cst = sem("s_cst")
        s_sp = sem("s_sp")
        s_sty = sem("s_sty")
        s_wsq = sem("s_wsq")
        s_dp = sem("s_dp")
        s_dvv = sem("s_dvv")
        s_dsq = sem("s_dsq")
        s_dco = sem("s_dco")
        s_wth = sem("s_wth")
        s_wtl = sem("s_wtl")
        s_xmh = sem("s_xmh")
        s_xml = sem("s_xml")
        s_cp = sem("s_cp")
        s_ce = sem("s_ce")
        s_cl = sem("s_cl")
        s_yh = sem("s_yh")
        s_yl = sem("s_yl")
        s_wr = sem("s_wr")
        s_idr = sem("s_idr")
        s_lg = sem("s_lg")
        s_ex = sem("s_ex")
        s_S = sem("s_S")
        s_pu = sem("s_pu")
        s_pl = sem("s_pl")
        s_rt = [sem(f"s_rt{i}") for i in range(4)]
        s_rp = sem("s_rp")
        s_l1 = sem("s_l1")
        s_lt = sem("s_lt")
        s_xt = [sem(f"s_xt{i}") for i in range(4)]
        s_it = sem("s_it")
        s_il = sem("s_il")
        s_hm = sem("s_hm")
        s_sl0 = sem("s_sl0")
        s_sq = sem("s_sq")
        s_oha = sem("s_oha")
        s_yd = [sem(f"s_yd{i}") for i in range(4)]
        s_o0 = sem("s_o0")
        s_s2t = sem("s_s2t")
        s_cnt = sem("s_cnt")
        s_cnt0 = sem("s_cnt0")
        s_pc0 = sem("s_pc0")
        s_m0 = sem("s_m0")
        s_rk0 = sem("s_rk0")
        s_pc = sem("s_pc")
        s_rr = sem("s_rr")
        s_off = sem("s_off")
        s_slot = sem("s_slot")
        s_slt = sem("s_slt")
        s_V = sem("s_V")
        s_v = sem("s_v")
        s_p = sem("s_p")
        s_R = sem("s_R")
        s_oh = sem("s_oh")
        s_im = sem("s_im")
        s_imc = sem("s_imc")
        s_idx = sem("s_idx")
        s_raw = [sem(f"s_raw{j}") for j in range(NJ)]
        s_w1h = sem("s_w1h")
        s_w1l = sem("s_w1l")
        s_w2h = sem("s_w2h")
        s_w2l = sem("s_w2l")
        s_A = sem("s_A")
        s_B = sem("s_B")
        s_Bt = sem("s_Bt")
        s_g = sem("s_g")
        s_hl = sem("s_hl")
        s_ev = sem("s_ev")
        s_bg = sem("s_bg")
        s_ob = sem("s_ob")
        s_sc = sem("s_sc")
        s_gat = [sem(f"s_gat{i}") for i in range(4)]
        s_xh = sem("s_xh")
        s_xl = sem("s_xl")
        s_b2 = [sem(f"s_b2{i}") for i in range(2)]

        block = ctx.enter_context(nc.Block())

        @block.sync
        def _(eng):
            eng.dma_start(AWT, affWT).then_inc(s_c["aff"], 16)
            eng.dma_start(cT[:, :, :], condT).then_inc(s_c["aff"], 16)
            eng.dma_start(affb[:, :], affbT).then_inc(s_c["aff"], 16)
            for c in range(4):
                eng.dma_start(WTraw[:, c, :], WT[:, c, :]).then_inc(s_wt[c], 16)
                eng.dma_start(XB[0][:, c, :], xT[0, :, c, :]).then_inc(s_x0[c], 16)
            eng.dma_start(XB[1], xT[1]).then_inc(s_x[1], 16)
            eng.dma_start(biasc[:, :], biasT).then_inc(s_c["bias"], 16)
            eng.dma_start(wr[:, :, :], WrT).then_inc(s_c["small"], 16)
            eng.dma_start(b1[:, :], b1T).then_inc(s_c["b1"], 16)

            def load_w(e, j):
                eng.dma_start(R[:, j, 0:512], W1[e, j]).then_inc(s_raw[j], 16)
                eng.dma_start(R[:, j, 512:1024], W2[e, j]).then_inc(s_raw[j], 16)

            def load_b2(e):
                eng.dma_start(B2[:, e % 2, :], b2[e:e + 1, :].broadcast_to([128, 512])).then_inc(s_b2[e % 2], 16)

            load_w(0, 0)
            load_w(0, 1)
            load_b2(0)
            load_b2(1)

            def y_rows(b):
                eng.wait_ge(s_pu, 4 * (b + 1))
                eng.wait_ge(s_pl, 4 * (b + 1))
                for t in range(4):
                    if b:
                        eng.wait_ge(s_yd[t], 16 * b)
                    eng.dma_start_transpose(XR[:, t, :].rearrange("p (k n) -> p k n", k=8),
                                            YP[b % 2][:, t, :, :].rearrange("p k n -> p (k n)")).then_inc(s_rt[t], 16)

            def y_store(b):
                for t in range(4):
                    n = 4 * b + t
                    eng.wait_ge(s_rt[t], 16 * (b + 1))
                    eng.dma_start(y_d[128 * n:128 * n + 128, :], XR[:, t, :]).then_inc(s_yd[t], 16)

            for b in range(2, NB):
                eng.wait_ge(s_xmh, 4 * (b - 1))
                eng.wait_ge(s_xml, 4 * (b - 1))
                eng.dma_start(XB[b % 2], xT[b]).then_inc(s_x[b % 2], 16)
                if b >= 3:
                    y_rows(b - 3)
                    y_store(b - 3)
            for b in (NB - 3, NB - 2):
                y_rows(b)
                y_store(b)
            eng.wait_ge(s_yh, 4 * NB)
            eng.wait_ge(s_yl, 4 * NB)
            y_rows(NB - 1)
            load_w(0, 2)
            y_store(NB - 1)
            for j in range(6, NJ):
                load_w(0, j)

            def transposes(u):
                for t in range(4):
                    n = 4 * (u - 1) + t
                    eng.wait_ge(s_gat[t], 16 * (u + 1))
                    if u:
                        eng.wait_ge(s_it, n + 1)
                        eng.wait_ge(s_il, n + 1)
                    eng.dma_start_transpose(XU[:, t, :, :], XR[:, t, :]).then_inc(s_xt[t], 16)

            transposes(0)
            for j in range(3, 6):
                load_w(0, j)
            for u in range(NU):
                if u + 1 < NU:
                    transposes(u + 1)
                if u % 2 and u + 1 < NU:
                    e = (u + 1) // 2
                    for j in range(NJ):
                        eng.wait_ge(s_w2h, 16 * u + j + 1)
                        eng.wait_ge(s_w2l, 16 * u + j + 1)
                        load_w(e, j)
                        if e >= 2 and j == 4:
                            eng.wait_ge(s_ev, 8 * (e - 1))
                            load_b2(e)
            for i in range(4):
                eng.wait_ge(s_yd[i], 16 * 8)
            eng.wait_ge(s_sc, 64 * NU)

        @block.gpsimd
        def _(eng):
            eng.memset(ident[:, :], 0.0).then_inc(s_p, 1)
            eng.wait_ge(s_p, 1)
            eng.affine_select(out=ident[:, :], in_=ident[:, :], compare_op=ALU.not_equal, fill=1.0,
                              base=0, pattern=[[-1, 128]], channel_multiplier=1).then_inc(s_id, 1)
            eng.memset(gtab[:, :], 0.0).then_inc(s_cst, 1)
            eng.iota(io128[:, :], pattern=[[1, 128]], base=0, channel_multiplier=0,
                     allow_small_or_imprecise_dtypes=True).then_inc(s_cst, 1)
            eng.iota(Jt[:, :], pattern=[[1, 128]], base=128, channel_multiplier=-1).then_inc(s_cst, 1)
            eng.iota(V[:, 0, :, :], pattern=[[0, 256]], base=0, channel_multiplier=1,
                     allow_small_or_imprecise_dtypes=True).then_inc(s_cst, 1)
            eng.iota(V[:, 1, :, :], pattern=[[128, NT], [0, 8]], base=0, channel_multiplier=0,
                     allow_small_or_imprecise_dtypes=True).then_inc(s_cst, 1)
            eng.memset(PS[:, :], 0.0).then_inc(s_p, 1)
            eng.wait_ge(s_p, 2)
            eng.affine_select(out=PS[:, :], in_=PS[:, :], compare_op=ALU.not_equal, fill=1.0,
                              base=0, pattern=[[-1, E]], channel_multiplier=1).then_inc(s_p, 1)
            eng.wait_ge(s_p, 3)
            eng.affine_select(out=PS[:, :], in_=PS[:, :], compare_op=ALU.not_equal, fill=1.0,
                              base=-E, pattern=[[-1, E]], channel_multiplier=1).then_inc(s_cst, 1)
            eng.memset(KR[:, :], 2.0 ** 64).then_inc(s_cst, 1)
            eng.memset(KC[:, 0:1], -float(K)).then_inc(s_cst, 1)
            eng.memset(ones[:, :], 1.0).then_inc(s_cst, 1)
            eng.memset(ON[:, :], 1.0).then_inc(s_cst, 1)
            eng.memset(OS[:, :], 2.0 ** 64).then_inc(s_cst, 1)
            eng.iota(J8[:, :], pattern=[[1, 8]], base=0, channel_multiplier=0).then_inc(s_cst, 1)
            eng.memset(kmag[:, 0, :], 2.0 ** 23).then_inc(s_cst, 1)
            eng.memset(kmag[:, 1, :], -1.0).then_inc(s_cst, 1)
            eng.memset(KC[:, 1:2], 0.5).then_inc(s_cst, 1)
            Sf = S[:, :, :].rearrange("p t e -> p (t e)")
            Vf = [V[:, i, :, :].rearrange("p t e -> p (t e)") for i in range(5)]
            eng.wait_ge(s_S, NB)
            for t in range(4):
                eng.wait_ge(s_rt[t], 16 * (NB - 1))
            eng.tensor_copy(Vf[2], Sf).then_inc(s_p, 1)
            eng.wait_ge(s_p, 4)
            eng.tensor_tensor(sr, Sf, Vf[2], ALU.subtract).then_inc(s_p, 1)
            eng.wait_ge(s_p, 5)
            eng.tensor_copy(Vf[3], sr).then_inc(s_p, 1)
            eng.wait_ge(s_p, 6)
            eng.tensor_tensor(sr2, sr, Vf[3], ALU.subtract).then_inc(s_p, 1)
            eng.wait_ge(s_p, 7)
            eng.tensor_copy(Vf[4], sr2).then_inc(s_V, 1)

            eng.wait_ge(s_hm, 1)
            eng.wait_ge(s_V, 1)
            eng.tensor_tensor(RH[:, :, :, :], V[:, :, :, 0:1].broadcast_to([128, 5, NT, 8]),
                              HM[:, None, :, :].broadcast_to([128, 5, NT, 8]), ALU.mult).then_inc(s_R, 1)

            def gather(u):
                eng.wait_ge(s_idx, u // 2 + 1)
                for t in range(4):
                    c = 4 * (u % 2) + t
                    if u:
                        eng.wait_ge(s_xt[t], 16 * u)
                    eng.indirect_dma_start(
                        XR[:, t, :], None, y_d[:, :],
                        bass.IndirectOffsetOnAxis(idx[:, u // 2, c:c + 1], 0),
                        bounds_check=NT * 128 - 1, oob_is_err=True).then_inc(s_gat[t], 16)

            def scatter(u):
                if u == 0:
                    eng.wait_ge(s_o0, 16)
                else:
                    eng.wait_ge(s_sc, 64 * u)
                for t in range(4):
                    c = 4 * (u % 2) + t
                    eng.wait_ge(s_ob, 4 * u + t + 1)
                    eng.indirect_dma_start(
                        out[:, :], bass.IndirectOffsetOnAxis(idx[:, u // 2, c:c + 1], 0),
                        OB[:, t, :], None,
                        bounds_check=NT * 128 - 1, oob_is_err=True,
                        compute_op=ALU.add).then_inc(s_sc, 16)

            for i in range(4):
                eng.wait_ge(s_yd[i], 16 * 8)
            gather(0)
            gather(1)
            eng.dma_start(out.rearrange("(a b) d -> a (b d)", a=512),
                          x.rearrange("(a b) d -> a (b d)", a=512)).then_inc(s_o0, 16)
            for u in range(NU):
                scatter(u)
                if u + 2 < NU:
                    gather(u + 2)

        @block.scalar
        def _(eng):

            def xm_hi(b, cs):
                eng.wait_ge(s_x[b % 2], 16 * ((b + 1) // 2))
                if b >= 2:
                    eng.wait_ge(s_cp, 4 * (b - 1))
                for c in cs:
                    eng.activation(XT[:, b % 2, 0, c, :], XB[b % 2][:, c, :], ACT.Copy,
                                   scale=sty[:, c, b:b + 1]).then_inc(s_xmh, 1)

            def evac(b, o):
                eng.wait_ge(s_cp, 4 * b + o + 1)
                if b >= 2:
                    eng.wait_ge(s_yl, 4 * (b - 1))
                eng.activation(YT[b % 2][:, o, :], BB[o][:, :], ACT.Identity,
                               scale=dco[:, o, b:b + 1], bias=biasc[:, o:o + 1]).then_inc(s_ce, 1)

            def y_hi(b, c):
                if b and c == 0:
                    eng.wait_ge(s_rp, b)
                eng.wait_ge(s_cl, 4 * b + c + 1)
                eng.activation(YH[:, c, :], YT[b % 2][:, c, :], ACT.Copy).then_inc(s_yh, 1)

            def upper(b, c):
                if b >= 2 and c == 0:
                    for t in range(4):
                        eng.wait_ge(s_rt[t], 16 * (b - 1))
                eng.wait_ge(s_cl, 4 * b + c + 1)
                eng.activation(planes(b, 0, c), words(b, c)[:, :, :, 1], ACT.Copy).then_inc(s_pu, 1)

            def l1(b):
                eng.wait_ge(s_rp, b + 1)
                if b:
                    eng.wait_ge(s_lt, b)
                eng.activation(L1[:, :], (TB, IB)[b % 2][0:2 * E, :], ACT.Copy).then_inc(s_l1, 1)

            def exps(b):
                eng.wait_ge(s_lg, b + 1)
                eng.activation(ex[:, :, :], lg[:, :, :], ACT.Exp).then_inc(s_ex, 1)

            for c in range(4):
                eng.wait_ge(s_wt[c], 16)
                eng.activation(wt(0, c), WTraw[:, c, :], ACT.Copy).then_inc(s_wth, 1)
                eng.wait_ge(s_sty, c + 1)
                eng.wait_ge(s_x0[c], 16)
                eng.activation(XT[:, 0, 0, c, :], XB[0][:, c, :], ACT.Copy,
                               scale=sty[:, c, 0:1]).then_inc(s_xmh, 1)
            eng.activation(WSQ, WTraw, ACT.Square).then_inc(s_wsq, 1)
            xm_hi(1, (0, 1, 2, 3))
            eng.wait_ge(s_c["small"], 16)
            eng.activation(RW[:, :, 0:E], wr[:, :, :], ACT.Copy).then_inc(s_wr, 1)
            eng.wait_ge(s_id, 1)
            eng.activation(IR[:, :], ident[:, :], ACT.Copy).then_inc(s_idr, 1)
            eng.wait_ge(s_dvv, 1)
            eng.activation(dsq[:, :, :], dv[:, :, :], ACT.Sqrt).then_inc(s_dsq, 1)
            eng.wait_ge(s_dco, 1)
            eng.wait_ge(s_c["bias"], 16)
            for b in range(NB):
                evac(b, 0)
                if b:
                    upper(b - 1, 2)
                    upper(b - 1, 3)
                evac(b, 1)
                if b:
                    l1(b - 1)
                if 0 < b < NB - 1:
                    xm_hi(b + 1, (0, 1))
                evac(b, 2)
                if b == 0:
                    evac(b, 3)
                for c in range(3):
                    y_hi(b, c)
                if 0 < b < NB - 1:
                    xm_hi(b + 1, (2, 3))
                if b:
                    exps(b - 1)
                    evac(b, 3)
                y_hi(b, 3)
                upper(b, 0)
                upper(b, 1)
            l1(NB - 1)
            upper(NB - 1, 2)
            upper(NB - 1, 3)
            exps(NB - 1)

            def w1_hi(i):
                j = i % NJ
                eng.wait_ge(s_raw[j], 32 * (i // 32 + 1))
                if i >= 3:
                    eng.wait_ge(s_A, i - 2)
                elif i < 3:
                    eng.wait_ge(s_cp, 4 * NB)
                eng.activation(W1S[:, i % 3, 0, :], R[:, j, 0:512], ACT.Copy).then_inc(s_w1h, 1)

            def w2_hi(i):
                j = i % NJ
                eng.wait_ge(s_raw[j], 32 * (i // 32 + 1))
                if i >= 3:
                    eng.wait_ge(s_B, i - 2)
                eng.activation(W2S[:, i % 3, 0, :], R[:, j, 512:1024], ACT.Copy).then_inc(s_w2h, 1)

            def x_upper(u, t):
                n = 4 * u + t
                eng.wait_ge(s_xt[t], 16 * (u + 1))
                if n >= 2:
                    eng.wait_ge(s_xl, n - 1)
                eng.activation(halves(n)[:, :, 1], XU[:, t, 0:4, :].rearrange("p c n -> p (c n)"),
                               ACT.Copy).then_inc(s_it, 1)

            def x_hi(u, t):
                n = 4 * u + t
                eng.wait_ge(s_it, n + 1)
                eng.wait_ge(s_il, n + 1)
                if u >= 2:
                    eng.wait_ge(s_A, NJ * (u - 1))
                eng.activation(XT[:, u % 2, 0, :, 128 * t:128 * t + 128],
                               XF[:, n % 2, :].rearrange("p (c n) -> p c n", c=4), ACT.Copy).then_inc(s_xh, 1)

            eng.wait_ge(s_cst, 5)
            eng.activation(gtab[:, :], gtab[:, :], ACT.Gelu)
            w1_hi(0)
            w1_hi(1)
            eng.wait_ge(s_sl0, 1)
            for k in range(8):
                last = eng.activation(SQ[:, 128 * k:128 * k + 128], io128[:, :], ACT.Square,
                                      bias=nsl0[:, 24 + k:25 + k])
            last.then_inc(s_sq, 1)
            eng.wait_ge(s_sq, 1)
            eng.activation(OH[:, 3, :, :].rearrange("p k n -> p (k n)"), SQ, ACT.Relu, scale=-1.0,
                           bias=1.0).then_inc(s_oha, 1)
            for t in range(4):
                x_upper(0, t)
                x_hi(0, t)
            for i in range(NBLK):
                if i + 2 < NBLK:
                    w1_hi(i + 2)
                w2_hi(i)
                eng.wait_ge(s_A, i + 1)
                if i >= 2:
                    eng.wait_ge(s_hl, i - 1)
                bias = b1[:, (i // 32) * NJ + i % NJ:(i // 32) * NJ + i % NJ + 1]
                if i == 0:
                    eng.wait_ge(s_c["b1"], 16)
                eng.activation(HF[:, i % 2, :], AB[i % 2][:, :], ACT.Gelu, bias=bias)
                eng.activation(HS[:, i % 3, 0, :], AB[i % 2][:, :], ACT.Gelu, bias=bias).then_inc(s_g, 1)
                u, j = i // NJ, i % NJ
                for t in range(4):
                    if u + 1 < NU and j == x_block(u, t) + 1:
                        x_hi(u + 1, t)
                for t in range(4):
                    if u + 1 < NU and j == x_block(u, t):
                        x_upper(u + 1, t)

        @block.vector
        def _(eng):
            chain = [0]

            def link(ins):
                chain[0] += 1
                ins.then_inc(s_v, 1)
                eng.wait_ge(s_v, chain[0])

            eng.wait_ge(s_c["aff"], 48)

            def style(c):
                eng.wait_ge(s_sp, c + 1)
                eng.scalar_tensor_tensor(sty[:, c, :], (TB, IB, *AB)[c][:, 0:8], 1.0 / 16.0,
                                         affb[:, c:c + 1].broadcast_to([128, NB]), ALU.mult, ALU.add).then_inc(s_sty, 1)


            def xm_lo_chunk(b, c):
                eng.wait_ge(s_xmh, 4 * b + c + 1)
                eng.scalar_tensor_tensor(XT[:, b % 2, 1, c, :], XB[b % 2][:, c, :], sty[:, c, b:b + 1],
                                         asf(XT[:, b % 2, 0, c, :]), ALU.mult, ALU.subtract).then_inc(s_xml, 1)

            for c in range(4):
                eng.wait_ge(s_wt[c], 16)
                eng.wait_ge(s_wth, c + 1)
                if c == 0:
                    style(0)
                eng.tensor_tensor(wt(1, c), WTraw[:, c, :], asf(wt(0, c)), ALU.subtract).then_inc(s_wtl, 1)
                if c == 0:
                    for k in range(1, 4):
                        style(k)
                    eng.wait_ge(s_sty, 4)
                eng.wait_ge(s_x0[c], 16)
                xm_lo_chunk(0, c)
                if c == 0:
                    eng.tensor_tensor(sty2[:, :, :], sty[:, :, :], sty[:, :, :], ALU.mult).then_inc(s_sty, 1)

            def xm_lo(b, cs):
                eng.wait_ge(s_x[b % 2], 16 * ((b + 1) // 2))
                for c in cs:
                    xm_lo_chunk(b, c)

            xm_lo(1, (0, 1, 2, 3))
            eng.wait_ge(s_cst, 15)
            link(eng.tensor_scalar(Jm[:, :], Jt[:, :], 7, None, ALU.bitwise_and))
            link(eng.tensor_scalar(BO[:, :], Jm[:, :], 0.0, None, ALU.is_equal))
            link(eng.scalar_tensor_tensor(TRI[:, :], Jt[:, :], 128.0, BO[:, :], ALU.is_gt, ALU.mult))

            link(eng.tensor_scalar(BOS[:, :], BO[:, :], 2.0 ** 64, None, ALU.mult))
            eng.tensor_scalar(DT[:, :], Jt[:, :], 128.0, -1.0, ALU.is_lt, ALU.mult)
            eng.memset(TT[:, 10, :], 0)
            eng.memset(sw0[:, :, :], 0.0)
            for m in range(10):
                last = eng.tensor_scalar(TT[:, m, :], J8[:, :], 27 - 3 * m, None, ALU.logical_shift_left)
            link(last)
            eng.wait_ge(s_wr, 1)
            eng.tensor_tensor(RW[:, :, E:2 * E], wr[:, :, :], asf(RW[:, :, 0:E]),
                              ALU.subtract).then_inc(s_wr, 1)

            eng.wait_ge(s_dp, 16)
            eng.tensor_scalar(dv[:, :, :], TB[:, 0:32].rearrange("p (c b) -> p c b", c=4), 1e-8, None,
                              ALU.add).then_inc(s_dvv, 1)
            eng.wait_ge(s_dsq, 1)
            link(eng.reciprocal(dr[:, :, :], dsq[:, :, :]))
            link(eng.tensor_tensor(de[:, :, :], dv[:, :, :], dr[:, :, :], ALU.mult))
            link(eng.tensor_tensor(de[:, :, :], de[:, :, :], dr[:, :, :], ALU.mult))
            link(eng.tensor_scalar(de[:, :, :], de[:, :, :], -0.5, 1.5, ALU.mult, ALU.add))
            eng.tensor_tensor(dco[:, :, :], dr[:, :, :], de[:, :, :], ALU.mult).then_inc(s_dco, 1)
            def clip(b, o):
                eng.wait_ge(s_ce, 4 * b + o + 1)
                yv = YT[b % 2][:, o, :]
                eng.tensor_scalar(yv, yv, -CLAMP, CLAMP, ALU.max, ALU.min).then_inc(s_cl, 1)

            def y_lo(b, c):
                eng.wait_ge(s_yh, 4 * b + c + 1)
                eng.tensor_tensor(YL[:, c, :], YT[b % 2][:, c, :], asf(YH[:, c, :]),
                                  ALU.subtract).then_inc(s_yl, 1)

            def lower(b, c):
                if b >= 2 and c == 0:
                    for t in range(4):
                        eng.wait_ge(s_rt[t], 16 * (b - 1))
                eng.wait_ge(s_cl, 4 * b + c + 1)
                eng.tensor_copy(planes(b, 1, c), words(b, c)[:, :, :, 0]).then_inc(s_pl, 1)

            def softmax(q):
                eng.wait_ge(s_lt, q + 1)
                lt = AB[q % 2][:, 0:4 * E].rearrange("p (t e) -> p t e", t=4)
                link(eng.tensor_reduce(mx[:, :], lt, AX.X, ALU.max))
                if q:
                    eng.wait_ge(s_ex, q)
                eng.tensor_tensor(lg[:, :, :], lt, mx[:, :, None].broadcast_to([128, 4, E]),
                                  ALU.subtract).then_inc(s_lg, 1)
                eng.wait_ge(s_ex, q + 1)
                link(eng.tensor_reduce(sm[:, :], ex[:, :, :], AX.X, ALU.add))
                link(eng.reciprocal(rs[:, :], sm[:, :]))
                eng.tensor_tensor(S[:, 4 * q:4 * q + 4, :], ex[:, :, :],
                                  rs[:, :, None].broadcast_to([128, 4, E]), ALU.mult).then_inc(s_S, 1)

            for b in range(NB):
                clip(b, 0)
                if b:
                    lower(b - 1, 2)
                    lower(b - 1, 3)
                clip(b, 1)
                if 0 < b < NB - 1:
                    xm_lo(b + 1, (0, 1))
                clip(b, 2)
                if b == 0:
                    clip(b, 3)
                for c in range(3):
                    y_lo(b, c)
                if 0 < b < NB - 1:
                    xm_lo(b + 1, (2, 3))
                if b:
                    softmax(b - 1)
                    clip(b, 3)
                y_lo(b, 3)
                lower(b, 0)
                lower(b, 1)
            lower(NB - 1, 2)
            lower(NB - 1, 3)
            eng.tensor_copy(C0[:, :], TT[:, 0, :])
            softmax(NB - 1)

            S0 = S[:, :, 0]
            eng.wait_ge(s_S, NB)
            C0f, CNf = C0[:, :].bitcast(f32), CN[:, :, :].bitcast(f32)
            for m in range(10):
                link(eng.tensor_tensor(ge0[:, :, :], S0[:, None, :].broadcast_to([128, 7, NT]),
                                       C0f[:, 1:8, None].broadcast_to([128, 7, NT]), ALU.is_ge))
                with nc.allow_low_precision(reason="counts up to 32 are exact"):
                    eng.tensor_reduce(cnt0[:, :], ge0[:, :, :], AX.X, ALU.add).then_inc(s_cnt0, 1)
                eng.tensor_tensor(CN[:, :, :], C0[:, :, None].broadcast_to([128, 8, 8]),
                                  TT[:, m + 1:m + 2, :].broadcast_to([128, 8, 8]), ALU.bitwise_or).then_inc(s_v, 1)
                chain[0] += 1
                eng.wait_ge(s_pc0, m + 1)
                eng.wait_ge(s_v, chain[0])
                link(eng.tensor_tensor(CNf[:, 1:8, :], (IB, AB[0])[m % 2][:, 0:7, None].broadcast_to([128, 7, 8]),
                                       CNf[:, 1:8, :], ALU.min))
                link(eng.tensor_reduce(C0f, CNf.rearrange("p i j -> p j i"), AX.X, ALU.max))
            eng.tensor_scalar(mge[:, 0, :], S0, C0f[:, 0:1], None, ALU.is_gt)
            eng.tensor_scalar(mge[:, 1, :], S0, C0f[:, 0:1], None, ALU.is_equal).then_inc(s_m0, 1)
            eng.wait_ge(s_rk0, 1)
            tot, rk = AB[1][:, 0:2 * NT], AB[1][:, 2 * NT:4 * NT]
            link(eng.tensor_tensor_scan(sc0[:, :], tot, sw0.rearrange("p k t -> p (k t)"), 0.0, ALU.add, ALU.add))
            link(eng.tensor_tensor(sw0[:, :, :].rearrange("p k t -> p (k t)"), sc0[:, :], rk, ALU.add))
            link(eng.tensor_tensor(sw0[:, :, :], sw0[:, :, :], mge[:, :, :], ALU.mult))
            link(eng.scalar_tensor_tensor(sl0[:, :], sw0[:, 0, :], -1.0, sw0[:, 1, :], ALU.add, ALU.add))
            eng.tensor_scalar(slo0[:, :], sl0[:, :], 127, None, ALU.bitwise_and)
            link(eng.tensor_scalar(shi0[:, :], sl0[:, :], 7, None, ALU.arith_shift_right))
            eng.tensor_scalar(nsl0[:, :], slo0[:, :], -1.0, None, ALU.mult).then_inc(s_sl0, 1)

            candf, cnextf = cand[:, :].bitcast(f32), cnext[:, :, :].bitcast(f32)

            def prepare():
                for k in range(4):
                    eng.memset(cand[:, k:k + 1], k << 28)
                eng.wait_ge(s_s2t, 1)
                link(eng.tensor_copy(S2[:, :], TB[:, 0:256]))
                link(eng.tensor_copy(S2h.bitcast(u16), S2[:, :].bitcast(u16)[:, 1::2]))

            def count(n):
                step = 1 << (28 - 2 * n)
                fine = step < 1 << 16
                for k in range(1, 4):
                    dst = (junk, sg, se)[k - 1]
                    last = eng.tensor_scalar(dst if fine else dst[:, 0:128].bitcast(bf16), S2[:, :] if fine else S2h, candf[:, k:k + 1], None, ALU.is_ge, ALU.add,
                                             accum_out=cnt[:, k - 1:k])
                last.then_inc(s_cnt, 1)
                for k in range(4):
                    last = eng.tensor_scalar(cnext[:, :, k], cand[:, :], k * (step >> 2), None, ALU.bitwise_or)
                last.then_inc(s_v, 1)
                chain[0] += 1

            def select(n):
                eng.wait_ge(s_pc, n + 1)
                eng.wait_ge(s_v, chain[0])
                link(eng.tensor_tensor(cnextf[:, 1:4, :], (IB, TB)[n % 2][:, 0:3, None].broadcast_to([128, 3, 4]),
                                       cnextf[:, 1:4, :], ALU.min))
                link(eng.tensor_reduce(candf, cnextf.rearrange("p i j -> p j i"), AX.X, ALU.max))

            thr = candf[:, 0:1]

            def ranks():
                for h in range(2):
                    q = slice(128 * h, 128 * h + 128)
                    eng.tensor_scalar(mg[:, q], S2[:, q], thr, None, ALU.is_gt, ALU.add, accum_out=r1[:, h:h + 1])
                    last = eng.tensor_scalar(me[:, q], S2[:, q], thr, None, ALU.is_equal, ALU.add,
                                             accum_out=r1[:, 2 + h:3 + h])
                last.then_inc(s_rr, 1)
                eng.wait_ge(s_rr, 1)
                for h in range(2):
                    q = slice(128 * h, 128 * h + 128)
                    eng.tensor_tensor_scan(sg[:, q], mg[:, q], mg[:, q], 0.0, ALU.add, ALU.max)
                    last = eng.tensor_tensor_scan(se[:, q], me[:, q], me[:, q], 0.0, ALU.add, ALU.max)
                link(last)

            def offsets():
                eng.wait_ge(s_off, 1)
                for h in range(2):
                    q = slice(128 * h, 128 * h + 128)
                    eng.scalar_tensor_tensor(sa[:, q], sg[:, q], IB[:, h:h + 1], mg[:, q], ALU.add, ALU.mult)
                    eng.scalar_tensor_tensor(sbq[:, q], se[:, q], IB[:, 2 + h:3 + h], me[:, q],
                                             ALU.add, ALU.mult).then_inc(s_slot, 1)

            def slots():
                eng.wait_ge(s_slt, 1)
                bits = TB[:, 0:256].bitcast(i32)
                eng.tensor_scalar(slo[:, :, :].rearrange("p t e -> p (t e)"), bits, 127, None, ALU.bitwise_and)
                link(eng.tensor_scalar(shi[:, :, :].rearrange("p t e -> p (t e)"), bits, 0x7FFFFF, 7,
                                       ALU.bitwise_and, ALU.arith_shift_right))

            def search(i):
                if 2 <= i <= 14:
                    select(i - 1)
                    count(i)
                if i == 15:
                    select(14)
                    ranks()
                if i == 16:
                    offsets()
                if i == 17:
                    slots()

            def build_rhs(e):
                if e:
                    eng.wait_ge(s_im, 4 * e)
                hi = shi[:, :, e:e + 1] if e else shi0[:, :, None]
                eng.tensor_tensor(HM[:, :, :], hi.broadcast_to([128, NT, 8]),
                                  io128[:, None, 0:8].broadcast_to([128, NT, 8]), ALU.is_equal).then_inc(s_hm, 1)
                if e == 0:
                    return
                eng.wait_ge(s_hm, e + 1)
                eng.tensor_tensor(RH[:, :, :, :], V[:, :, :, e:e + 1].broadcast_to([128, 5, NT, 8]),
                                  HM[:, None, :, :].broadcast_to([128, 5, NT, 8]), ALU.mult).then_inc(s_R, 1)

            def build_oh(e, q):
                if e:
                    eng.wait_ge(s_im, 4 * e)
                eng.tensor_tensor(OH[:, q, :, :],
                                  (slo[:, 8 * q:8 * q + 8, e:e + 1] if e else
                                   slo0[:, 8 * q:8 * q + 8, None]).broadcast_to([128, 8, 128]),
                                  io128[:, None, :].broadcast_to([128, 8, 128]), ALU.is_equal).then_inc(s_oh, 1)

            def finish_idx(e):
                eng.wait_ge(s_im, 4 * e + 4)
                v = IB[:, 0:40].rearrange("p (v h) -> p h v", v=5)
                with nc.allow_low_precision(reason="token numbers below 4096 are exact"):
                    eng.tensor_reduce(idx[:, e, :], v[:, :, 0:2], AX.X, ALU.add).then_inc(s_idx, 1)
                eng.tensor_reduce(G[:, e, :], v[:, :, 2:5], AX.X, ALU.add).then_inc(s_imc, 1)

            build_rhs(0)
            for q in range(3):
                build_oh(0, q)
            finish_idx(0)

            def w1_lo(i):
                eng.wait_ge(s_w1h, i + 1)
                eng.tensor_tensor(W1S[:, i % 3, 1, :], R[:, i % NJ, 0:512], asf(W1S[:, i % 3, 0, :]),
                                  ALU.subtract).then_inc(s_w1l, 1)

            def w2_lo(i):
                eng.wait_ge(s_w2h, i + 1)
                eng.tensor_tensor(W2S[:, i % 3, 1, :], R[:, i % NJ, 512:1024], asf(W2S[:, i % 3, 0, :]),
                                  ALU.subtract).then_inc(s_w2l, 1)

            def x_lower(u, t):
                n = 4 * u + t
                eng.wait_ge(s_xt[t], 16 * (u + 1))
                if n >= 2:
                    eng.wait_ge(s_xh, n - 1)
                    eng.wait_ge(s_xl, n - 1)
                eng.tensor_copy(halves(n)[:, :, 0], XU[:, t, 4:8, :].rearrange("p c n -> p (c n)")).then_inc(s_il, 1)

            def x_lo(u, t):
                n = 4 * u + t
                eng.wait_ge(s_xh, n + 1)
                q = slice(128 * t, 128 * t + 128)
                eng.tensor_tensor(XT[:, u % 2, 1, :, q], XF[:, n % 2, :].rearrange("p (c n) -> p c n", c=4),
                                  asf(XT[:, u % 2, 0, :, q]), ALU.subtract).then_inc(s_xl, 1)

            def evac_add(u):
                e = u // 2
                eng.wait_ge(s_b2[e % 2], 16 * (e // 2 + 1))
                if u:
                    eng.wait_ge(s_sc, 64 * u)
                for t in range(4):
                    if t < 3:
                        eng.wait_ge(s_Bt, 3 * u + t + 1)
                    else:
                        eng.wait_ge(s_B, NJ * (u + 1))
                    if u == NU - 1 and t == 3:
                        eng.wait_ge(s_bg, 1)
                        eng.scalar_tensor_tensor(OB[:, t, :], BB[t][:, :], G[:, e, 7:8], BG[:, :],
                                                 ALU.mult, ALU.add).then_inc(s_ob, 1)
                        continue
                    eng.tensor_tensor(OB[:, t, :], BB[t][:, :], B2[:, e % 2, :], ALU.add).then_inc(s_ev, 1)
                    if u == NU - 1:
                        evac_mul(u, t)

            def evac_mul(u, t):
                e = u // 2
                eng.wait_ge(s_imc, e + 1)
                c = 4 * (u % 2) + t
                eng.wait_ge(s_ev, 4 * u + t + 1)
                eng.tensor_scalar(OB[:, t, :], OB[:, t, :], G[:, e, c:c + 1], None, ALU.mult).then_inc(s_ob, 1)

            w1_lo(0)
            w1_lo(1)
            prepare()
            count(0)
            select(0)
            count(1)
            x_lower(0, 0)
            for t in range(3):
                x_lower(0, t + 1)
                x_lo(0, t)
            x_lo(0, 3)
            for i in range(NBLK + 2):
                if i + 2 < NBLK:
                    w1_lo(i + 2)
                if i < NBLK:
                    w2_lo(i)
                    eng.wait_ge(s_g, i + 1)
                    eng.tensor_tensor(HS[:, i % 3, 1, :], HF[:, i % 2, :], asf(HS[:, i % 3, 0, :]),
                                      ALU.subtract).then_inc(s_hl, 1)
                search(i)
                if i == NBLK - 1:
                    eng.tensor_scalar(BG[:, :], B2[:, 1, :], G[:, E - 1, 7:8], None, ALU.mult).then_inc(s_bg, 1)
                u, j = i // NJ, i % NJ
                if u >= 1 and j == 1:
                    evac_add(u - 1)
                if u >= 1 and j == 2 and i < NBLK:
                    for t in range(4):
                        evac_mul(u - 1, t)
                for t in range(4):
                    if u + 1 < NU and j == x_block(u, t) + 1:
                        x_lo(u + 1, t)
                for t in range(4):
                    if u + 1 < NU and j == x_block(u, t):
                        x_lower(u + 1, t)
                if u == 1:
                    if j == 3:
                        build_rhs(1)
                    if 4 <= j <= 7:
                        build_oh(1, j - 4)
                    if j == 9:
                        finish_idx(1)
                if u % 2 == 0 and 0 < u < NU - 2:
                    e = u // 2 + 1
                    if j == 3:
                        build_rhs(e)
                    if j in (3, 5, 7, 9):
                        build_oh(e, (j - 3) // 2)
                    if j == 13:
                        finish_idx(e)

        @block.tensor
        def _(eng):
            mm = nc.tensor.matmul
            eng.wait_ge(s_c["aff"], 48)
            for c in range(4):
                for k in range(2):
                    last = mm((TB, IB, *AB)[c][:, 0:8], AWT[:, k, 128 * c:128 * c + 128], cT[:, k, :],
                              start=(k == 0), stop=(k == 1))
                last.then_inc(s_sp, 1)
            eng.wait_ge(s_id, 1)
            for n in range(3):
                mm(BB[0][:, 0:128], ident[:, :], ident[:, :], start=True, stop=True)

            def demod(n):
                o, c = n // 4, n % 4
                if n == 0:
                    eng.wait_ge(s_wsq, 1)
                    eng.wait_ge(s_sty, 5)
                mm(TB[:, 8 * o:8 * o + 8], WSQ[:, c, 128 * o:128 * o + 128], sty2[:, c, :],
                   start=(c == 0), stop=(c == 3)).then_inc(s_dp, 1)

            def cond(b, o, cs):
                if b and cs[0] == 0:
                    eng.wait_ge(s_ce, 4 * (b - 1) + o + 1)
                for c in cs:
                    if o == 0:
                        eng.wait_ge(s_xmh, 4 * b + c + 1)
                        eng.wait_ge(s_xml, 4 * b + c + 1)
                    for n, (a, d) in enumerate(((0, 0), (0, 1), (1, 0))):
                        last = mm(BB[o][:, :], wt(a, c)[:, 128 * o:128 * o + 128], XT[:, b % 2, d, c, :],
                                  start=(c == 0 and n == 0), stop=(c == 3 and n == 2))
                if cs[-1] == 3:
                    last.then_inc(s_cp, 1)

            def cond0():
                for c in range(4):
                    eng.wait_ge(s_xmh, c + 1)
                    eng.wait_ge(s_wtl, c + 1)
                    eng.wait_ge(s_xml, c + 1)
                    for o in range(4):
                        for n, (a, d) in enumerate(((0, 0), (0, 1), (1, 0))):
                            last = mm(BB[o][:, :], wt(a, c)[:, 128 * o:128 * o + 128], XT[:, 0, d, c, :],
                                      start=(c == 0 and n == 0), stop=(c == 3 and n == 2))
                            k = 12 * (c - 2) + 3 * o + n
                            if 0 <= k < 16:
                                demod(k)
                        if c == 3:
                            last.then_inc(s_cp, 1)

            def router(b):
                if b == 0:
                    eng.wait_ge(s_wr, 2)
                    eng.wait_ge(s_dvv, 1)
                if b >= 2:
                    eng.wait_ge(s_l1, b - 1)
                for c in range(4):
                    eng.wait_ge(s_yh, 4 * b + c + 1)
                    eng.wait_ge(s_yl, 4 * b + c + 1)
                    for n, Y in enumerate((YH, YL)):
                        last = mm((TB, IB)[b % 2][0:2 * E, :], RW[:, c, :], Y[:, c, :],
                                  start=(c == 0 and n == 0), stop=(c == 3 and n == 1))
                last.then_inc(s_rp, 1)

            def router_t(b):
                if b == 0:
                    eng.wait_ge(s_cst, 15)
                if b >= 2:
                    eng.wait_ge(s_lg, b - 1)
                eng.wait_ge(s_l1, b + 1)
                for t in range(4):
                    last = mm(AB[b % 2][:, E * t:E * t + E], L1[:, 128 * t:128 * t + 128], PS[:, :],
                              start=True, stop=True)
                last.then_inc(s_lt, 1)

            cond0()
            for b in range(1, NB):
                cond(b, 0, (0, 1, 2, 3))
                cond(b, 1, (0, 1, 2, 3))
                router(b - 1)
                cond(b, 2, (0, 1, 2, 3))
                router_t(b - 1)
                cond(b, 3, (0, 1, 2, 3))
            router(NB - 1)
            router_t(NB - 1)
            for m in range(10):
                pc = (IB, AB[0])[m % 2][:, 0:7]
                for i in range(2):
                    mm(pc, KR[:, :], KC[:, i:i + 1].broadcast_to([1, 7]), start=(i == 0), stop=False)
                eng.wait_ge(s_cnt0, m + 1)
                mm(pc, OS[:, :], cnt0[:, :], start=False, stop=True).then_inc(s_pc0, 1)
            eng.wait_ge(s_m0, 1)
            mk = mge[:, :, :].rearrange("p k t -> p (k t)")
            mm(AB[1][:, 0:2 * NT], ON[:, :], mk, start=True, stop=True)
            mm(AB[1][:, 2 * NT:4 * NT], DT[:, :], mk, start=True, stop=True).then_inc(s_rk0, 1)

            def to_rows():
                for h in range(2):
                    last = nc.tensor.transpose(TB[:, 128 * h:128 * h + 128],
                                               S[:, 16 * h:16 * h + 16, :].rearrange("p t e -> p (t e)"),
                                               ident[:, :])
                last.then_inc(s_s2t, 1)

            def count(n):
                if n == 0:
                    eng.wait_ge(s_imc, 1)
                pc = (IB, TB)[n % 2][:, 0:3]
                for i in range(2):
                    mm(pc, KR[:, :], KC[:, i:i + 1].broadcast_to([1, 3]), start=(i == 0), stop=False)
                eng.wait_ge(s_cnt, n + 1)
                mm(pc, BOS[:, :], cnt[:, :], start=False, stop=True).then_inc(s_pc, 1)

            def offsets():
                eng.wait_ge(s_rr, 1)
                mm(IB[:, 0:4], TRI[:, :], r1[:, 0:4], start=True, stop=False)
                mm(IB[:, 1:4:2], BO[:, :], r1[:, 0:4:2], start=False, stop=False)
                mm(IB[:, 2:4], BO[:, :], r1[:, 0:1].broadcast_to([128, 2]), start=False, stop=False)
                mm(IB[:, 2:4], BO[:, :], r1[:, 1:2].broadcast_to([128, 2]), start=False, stop=True).then_inc(s_off, 1)

            def slots():
                for h in range(2):
                    for n in range(2):
                        mm(TB[:, 128 * h:128 * h + 128], ones[:, :], kmag[:, n, :], start=(n == 0), stop=False)
                    eng.wait_ge(s_slot, h + 1)
                    for n, v in enumerate((sa, sbq)):
                        last = mm(TB[:, 128 * h:128 * h + 128], v[:, 128 * h:128 * h + 128], IR[:, :],
                                  start=False, stop=(n == 1))
                last.then_inc(s_slt, 1)

            def search(i):
                if 3 <= i <= 15:
                    count(i - 1)
                if i == 16:
                    offsets()
                if i == 17:
                    slots()

            def lists(e, q):
                if q == 0:
                    eng.wait_ge(s_R, e + 1)
                    if e:
                        eng.wait_ge(s_imc, e)
                if (e, q) == (0, 3):
                    eng.wait_ge(s_oha, 1)
                else:
                    eng.wait_ge(s_oh, 4 * e + q + (e == 0))
                for k in range(8):
                    t = 8 * q + k
                    last = mm(IB[:, 0:40].rearrange("p (v h) -> p v h", v=5), OH[:, q, :, :][:, k, :],
                              RH[:, :, t, :], start=(t == 0), stop=(t == NT - 1))
                last.then_inc(s_im, 1)

            def all_lists(e):
                for q in range(4):
                    lists(e, q)

            def A(i):
                u = i // NJ
                if i % NJ == 0:
                    eng.wait_ge(s_xh, 4 * u + 4)
                    eng.wait_ge(s_xl, 4 * u + 4)
                if i >= 2:
                    eng.wait_ge(s_g, i - 1)
                eng.wait_ge(s_w1h, i + 1)
                eng.wait_ge(s_w1l, i + 1)
                for c in range(4):
                    for n, (a, d) in enumerate(((0, 0), (0, 1), (1, 0))):
                        last = mm(AB[i % 2][:, :], W1S[:, i % 3, a, 128 * c:128 * c + 128], XT[:, u % 2, d, c, :],
                                  start=(c == 0 and n == 0), stop=(c == 3 and n == 2))
                last.then_inc(s_A, 1)

            def A_pair(i, t):
                eng.wait_ge(s_xh, t + 2)
                eng.wait_ge(s_w1h, i + 1)
                eng.wait_ge(s_w1l, i + 1)
                q = slice(128 * t, 128 * t + 256)
                order = [(c, a, 0) for c in range(4) for a in range(2)] + [(c, 0, 1) for c in range(4)]
                for n, (c, a, d) in enumerate(order):
                    if n == 8:
                        eng.wait_ge(s_xl, t + 2)
                    last = mm(AB[i][:, q], W1S[:, i, a, 128 * c:128 * c + 128], XT[:, 0, d, c, q],
                              start=(n == 0), stop=(n == 11))
                if t == 2:
                    last.then_inc(s_A, 1)

            def B_last():
                for i in (NBLK - 2, NBLK - 1):
                    eng.wait_ge(s_w2h, i + 1)
                    eng.wait_ge(s_w2l, i + 1)
                    eng.wait_ge(s_g, i + 1)
                    eng.wait_ge(s_hl, i + 1)
                for t in range(4):
                    for i in (NBLK - 2, NBLK - 1):
                        for n, (a, d) in enumerate(((0, 0), (0, 1), (1, 0))):
                            last = mm(BB[t][:, :], HS[:, i % 3, a, 128 * t:128 * t + 128], W2S[:, i % 3, d, :],
                                      start=False, stop=(i == NBLK - 1 and n == 2))
                    if t < 3:
                        last.then_inc(s_Bt, 1)
                last.then_inc(s_B, 2)

            def B(i):
                u, j = i // NJ, i % NJ
                eng.wait_ge(s_w2h, i + 1)
                eng.wait_ge(s_w2l, i + 1)
                eng.wait_ge(s_g, i + 1)
                eng.wait_ge(s_hl, i + 1)
                for t in range(4):
                    if j == 0 and u:
                        eng.wait_ge(s_ev, 4 * (u - 1) + t + 1)
                    for n, (a, d) in enumerate(((0, 0), (0, 1), (1, 0))):
                        last = mm(BB[t][:, :], HS[:, i % 3, a, 128 * t:128 * t + 128], W2S[:, i % 3, d, :],
                                  start=(j == 0 and n == 0), stop=(j == NJ - 1 and n == 2))
                    if j == NJ - 1 and t < 3:
                        last.then_inc(s_Bt, 1)
                last.then_inc(s_B, 1)

            for q in range(4):
                lists(0, q)
            to_rows()
            for n in range(2):
                count(n)
            for n in range(14):
                mm(AB[0][:, :], IR[:, :], YH[:, n % 4, :], start=True, stop=True)
            for t in (0, 2):
                A_pair(0, t)
                A_pair(1, t)
            for i in range(2, NBLK + 1):
                if i < NBLK:
                    A(i)
                search(i)
                u, j = i // NJ, i % NJ
                if u % 2 == 0 and 0 < u < NU - 2 and j == 11:
                    all_lists(u // 2 + 1)
                if u == 1 and j == 8:
                    all_lists(1)
                if i == NBLK:
                    B_last()
                else:
                    B(i - 2)


_OUT = (8, 512, 512)


def kernel(x, cond_512, L0_cond_weight, L0_cond_bias, L0_cond_affine_w, L0_cond_affine_b, L0_ffn_Wr,
           L0_ffn_W1, L0_ffn_b1, L0_ffn_W2, L0_ffn_b2):
    import numpy as np
    import concourse.bacc as bacc
    from concourse import mybir
    from concourse.bass_utils import run_bass_kernel_spmd

    def chunks(a, n):
        a = np.asarray(a)
        return np.ascontiguousarray(a.reshape(n, 128, -1).transpose(1, 0, 2))

    x = np.asarray(x)
    arrays = {
        "xT": np.ascontiguousarray(x.reshape(8, 512, 4, 128).transpose(0, 3, 2, 1)),
        "x": np.ascontiguousarray(x.reshape(4096, 512)),
        "condT": chunks(np.asarray(cond_512).T, 2),
        "WT": chunks(np.asarray(L0_cond_weight).T, 4),
        "biasT": np.ascontiguousarray(np.asarray(L0_cond_bias).reshape(4, 128).T),
        "affWT": chunks(np.asarray(L0_cond_affine_w).T, 2),
        "affbT": np.ascontiguousarray(np.asarray(L0_cond_affine_b).reshape(4, 128).T),
        "WrT": chunks(L0_ffn_Wr, 4),
        "W1": np.ascontiguousarray(
            np.asarray(L0_ffn_W1).reshape(8, 4, 128, 16, 128).transpose(0, 3, 2, 1, 4)).reshape(8, 16, 128, 512),
        "b1T": np.ascontiguousarray(np.asarray(L0_ffn_b1).reshape(8, 16, 128).transpose(2, 0, 1)).reshape(128, 128),
        "W2": np.ascontiguousarray(np.asarray(L0_ffn_W2).reshape(8, 16, 128, 512)),
        "b2": np.ascontiguousarray(np.asarray(L0_ffn_b2)),
    }
    nc = bacc.Bacc("TRN2", target_bir_lowering=False, num_devices=1)
    f32 = mybir.dt.float32
    args = {n: nc.dram_tensor(f"in_{n}", a.shape, f32, kind="ExternalInput").ap() for n, a in arrays.items()}
    out = nc.dram_tensor("out_0", (4096, 512), f32, kind="ExternalOutput").ap()
    adaln_moe_kernel(nc, out=out, **args)
    r = run_bass_kernel_spmd(nc, [{f"in_{n}": a for n, a in arrays.items()}], core_ids=[0])
    return r.results[0]["out_0"].reshape(_OUT)
```
